# Optimizing a Trainium2 kernel written in Bass

```python
import numpy as np
import jax
import jax.numpy as jnp

def _softmax(x, axis=-1):
    return jax.nn.softmax(x, axis=axis)

def _gelu(x):
    return jax.nn.gelu(x, approximate=True)

def _silu(x):
    return jax.nn.silu(x)

def _sigmoid(x):
    return jax.nn.sigmoid(x)

def _layernorm(x, axis=-1, eps=1e-05):
    m = jnp.mean(x, axis=axis, keepdims=True)
    v = jnp.var(x, axis=axis, keepdims=True)
    return (x - m) / jnp.sqrt(v + eps)

def _scatter_add(tgt, idx, src, axis=0):
    return tgt.at[idx].add(src)

def _segment_sum(src, seg, n):
    return jax.ops.segment_sum(src, seg, n)
kernel_name = 'mk_prb_d1_jaxref_r2_206248'

def setup_inputs(seed: int=0):
    np.random.seed(seed)
    _w = jnp.asarray

    def _L0_attn_setup():
        import jax, jax.numpy as jnp
        import numpy as np
        B, L, E, H = (4, 2048, 512, 16)
        D = E // H
        EPS = 0.0001
        key = jax.random.key(seed)
        k1, k2, k3 = jax.random.split(key, 3)
        x = jax.random.normal(k1, (B, L, E), dtype=jnp.float32)
        W_qkv = jax.random.normal(k2, (E, 3 * E), dtype=jnp.float32) * (1.0 / np.sqrt(E))
        b_qkv = jnp.zeros((3 * E,), dtype=jnp.float32)
        W_out = jax.random.normal(k3, (E, E), dtype=jnp.float32) * (1.0 / np.sqrt(E))
        b_out = jnp.zeros((E,), dtype=jnp.float32)
        return {'x': x, 'W_qkv': W_qkv, 'b_qkv': b_qkv, 'W_out': W_out, 'b_out': b_out}
    _L0_attn_in = _L0_attn_setup()

    def _L0_ffn_setup():
        import jax, jax.numpy as jnp
        import numpy as np
        N_EXPERT_CAPACITY = 2
        key = jax.random.key(seed)
        k1, k2, k3, k4 = jax.random.split(key, 4)
        B, S, D, E, F = (8, 512, 512, 8, 1024)
        x = jax.random.normal(k1, (B, S, D), dtype=jnp.float32)
        choice_w = jax.random.uniform(k2, (E, D), dtype=jnp.float32, minval=-1.0, maxval=1.0) * (1.0 / np.sqrt(D))
        w1 = jax.random.uniform(k3, (E, D, F), dtype=jnp.float32, minval=-1.0, maxval=1.0) * (1.0 / np.sqrt(D))
        w2 = jax.random.uniform(k4, (E, F, D), dtype=jnp.float32, minval=-1.0, maxval=1.0) * (1.0 / np.sqrt(F))
        return {'x': x, 'choice_w': choice_w, 'w1': w1, 'w2': w2}
    _L0_ffn_in = _L0_ffn_setup()
    _d = {'L0_attn_x': _L0_attn_in['x'], 'L0_attn_W_qkv': _L0_attn_in['W_qkv'], 'L0_attn_b_qkv': _L0_attn_in['b_qkv'], 'L0_attn_W_out': _L0_attn_in['W_out'], 'L0_attn_b_out': _L0_attn_in['b_out'], 'L0_ffn_choice_w': _L0_ffn_in['choice_w'], 'L0_ffn_w1': _L0_ffn_in['w1'], 'L0_ffn_w2': _L0_ffn_in['w2']}
    _x0 = _d['L0_attn_x']
    _d['L0_attn_x'] = jax.random.normal(jax.random.fold_in(jax.random.key(seed), 1), (2, 4096, 512), dtype=_x0.dtype)
    del _x0
    return _d

def reference(L0_attn_x, L0_attn_W_qkv, L0_attn_b_qkv, L0_attn_W_out, L0_attn_b_out, L0_ffn_choice_w, L0_ffn_w1, L0_ffn_w2):

    def _L0_attn_ref(x, W_qkv, b_qkv, W_out, b_out):
        import jax, jax.numpy as jnp
        import numpy as np
        B, L, E, H = (4, 2048, 512, 16)
        D = E // H
        EPS = 0.0001
        Bb, Ll, Ee = x.shape
        qkv = x @ W_qkv + b_qkv
        q, k, v = jnp.split(qkv, 3, axis=-1)
        q = q.reshape(Bb, Ll, H, D).transpose(0, 2, 1, 3)
        k = k.reshape(Bb, Ll, H, D).transpose(0, 2, 1, 3)
        v = v.reshape(Bb, Ll, H, D).transpose(0, 2, 1, 3)
        positions = jnp.arange(Ll, dtype=jnp.float32).reshape(1, 1, Ll, 1)
        cos_w = jnp.cos(jnp.pi / 2 * positions / Ll)
        sin_w = jnp.sin(jnp.pi / 2 * positions / Ll)
        q_prime = jax.nn.relu(q)
        k_prime = jax.nn.relu(k)
        q_cos, q_sin = (q_prime * cos_w, q_prime * sin_w)
        k_cos, k_sin = (k_prime * cos_w, k_prime * sin_w)
        kv_cos = jnp.einsum('bhld,bhle->bhde', k_cos, v)
        kv_sin = jnp.einsum('bhld,bhle->bhde', k_sin, v)
        context = jnp.einsum('bhld,bhde->bhle', q_cos, kv_cos) + jnp.einsum('bhld,bhde->bhle', q_sin, kv_sin)
        k_cos_sum = k_cos.sum(axis=2)
        k_sin_sum = k_sin.sum(axis=2)
        norm = jnp.einsum('bhld,bhd->bhl', q_cos, k_cos_sum) + jnp.einsum('bhld,bhd->bhl', q_sin, k_sin_sum)
        output = context / (norm[..., None] + EPS)
        output = output.transpose(0, 2, 1, 3).reshape(Bb, Ll, Ee)
        return output @ W_out + b_out

    def _L0_ffn_ref(x, choice_w, w1, w2):
        import jax, jax.numpy as jnp
        import numpy as np
        N_EXPERT_CAPACITY = 2
        B, S, D = x.shape
        E = choice_w.shape[0]
        k = S * N_EXPERT_CAPACITY // E
        probs = jax.nn.softmax(jnp.einsum('bsd,ed->bse', x, choice_w), axis=-1)
        G, I = jax.lax.top_k(jnp.swapaxes(probs, -1, -2), k)
        x_in = jnp.take_along_axis(x[:, None, :, :], I[..., None], axis=2)
        h = jax.nn.silu(jnp.einsum('bekd,edf->bekf', x_in, w1))
        x_mlp = jnp.einsum('bekf,efd->bekd', h, w2)
        b_idx = jnp.arange(B)[:, None, None]
        out = jnp.zeros_like(x).at[b_idx, I].add(G[..., None] * x_mlp)
        return out
    x = L0_attn_x
    xn = _layernorm(x, axis=-1)
    x = x + _L0_attn_ref(xn, L0_attn_W_qkv, L0_attn_b_qkv, L0_attn_W_out, L0_attn_b_out) + _L0_ffn_ref(xn, L0_ffn_choice_w, L0_ffn_w1, L0_ffn_w2)
    return x

_drawn_inputs = setup_inputs


def setup_inputs(seed=0):
    import zlib

    import numpy as np

    out = dict(_drawn_inputs(seed))
    spreads = {'L0_attn_b_qkv': (0.0, 0.1), 'L0_attn_b_out': (0.0, 0.1)}
    factors = {}
    for name, (base, spread) in spreads.items():
        noise = np.random.default_rng([zlib.crc32(name.encode()), seed]).standard_normal(out[name].shape)
        drawn = base * np.exp(spread * noise) if base else spread * noise
        out[name] = jnp.asarray(drawn.astype(out[name].dtype))
    for name, factor in factors.items():
        out[name] = (out[name] * factor).astype(out[name].dtype)
    return out
```

```python
from contextlib import ExitStack

import numpy as np

import concourse.bass as bass
from concourse import mybir

ALU = mybir.AluOpType
ACT = mybir.ActivationFunctionType
AX = mybir.AxisListType
F32 = mybir.dt.float32
F32R = mybir.dt.float32r
BF16 = mybir.dt.bfloat16
I32 = mybir.dt.int32

P = 128
B, L, D = 2, 4096, 512
H, HD = 16, 32
E, F = 8, 1024
CAP = L * 2 // E
KD = D // P
G = KD
HPG = P // HD
KF = F // P
BLK = 512
TPB = BLK // P
NBLK = L // BLK
NT = L // P
ROW = D + E
LN_EPS = 1e-5
NORM_EPS = 1e-4
UNITS = B * CAP // BLK
HALVES = CAP // BLK
SLOT_TILES = CAP // P
BITS = 30
VW = P + 2
CON_LOADS = 6 + KD
ROUTE = BITS + 4

C_IDENT, C_BLOCK, C_LOWER, C_IOTA, C_COS, C_SIN, C_EIGHT, C_TILE, C_PCOL, C_HEAD, C_END = np.cumsum(
    [0, P, P, P, P, NT, NT, 8, NT, 1, HPG]).tolist()


def constants():
    p = np.arange(P)
    c = np.zeros((P, C_END), np.float32)
    same = p[:, None] // NT == p[None, :] // NT
    c[:, C_IDENT:C_BLOCK] = np.eye(P)
    c[:, C_BLOCK:C_LOWER] = same
    c[:, C_LOWER:C_IOTA] = same & (p[:, None] < p[None, :])
    c[:, C_IOTA:C_COS] = p[None, :]
    angle = (np.float32(np.pi / 2) * np.arange(L, dtype=np.float32) / np.float32(L)).reshape(NT, P).T
    c[:, C_COS:C_SIN] = np.cos(angle)
    c[:, C_SIN:C_EIGHT] = np.sin(angle)
    c[:, C_EIGHT:C_TILE] = np.arange(8)
    c[:, C_TILE:C_PCOL] = np.arange(NT)
    c[:, C_PCOL] = p
    c[:, C_HEAD:C_END] = p[:, None] // HD == np.arange(HPG)[None, :]
    bits = np.zeros((P, NT), np.int32)
    bits[:, :BITS] = 1 << np.arange(BITS - 1, -1, -1)
    return c, bits


class Steps:

    def __init__(self, eng, sem):
        self.eng, self.sem, self.base, self.n, self.outer = eng, sem, 0, 0, []

    def did(self, ins):
        ins.then_inc(self.sem, 1)
        self.n += 1

    def wait(self):
        self.eng.wait_ge(self.sem, self.base + self.n)

    def enter(self, turn, per_turn):
        self.outer.append((self.base, self.n, per_turn))
        self.base, self.n = self.base + self.n + turn * per_turn, 0

    def leave(self, turns):
        base, n, per_turn = self.outer.pop()
        assert self.n == per_turn, f"{self.n} steps in a body of {per_turn}"
        self.base, self.n = base, n + turns * per_turn


def build(nc, x, w_qkv, b_qkv, w_out, b_out, choice_w, w1, w2, consts, bits, out, scratch):
    xf = x.rearrange("b l d -> (b l) d")
    of = out.rearrange("b l d -> (b l) d")
    with ExitStack() as ctx:
        def sem(name):
            return ctx.enter_context(nc.semaphore(name))

        def keep(name, shape, dt=F32):
            return ctx.enter_context(nc.sbuf_tensor(name, shape, dt))

        ps = ctx.enter_context(nc.psum_tensor("ps", [P, 8, 512], F32))

        con = keep("con", [P, C_END])
        bit = keep("bit", [P, NT], I32)
        rank_lo = keep("rank_lo", [P, B, E + 1, NT], BF16)
        rank_hi = keep("rank_hi", [P, B, E + 1, NT], BF16)
        iota_bf = keep("iota_bf", [P, P], BF16)
        zero = keep("zero", [P, 2 * VW], BF16)
        ident = con[:, C_IDENT:C_BLOCK]
        same_block = con[:, C_BLOCK:C_LOWER]
        earlier = con[:, C_LOWER:C_IOTA]

        with ExitStack() as early:
            def sb(name, shape, dt=F32):
                return early.enter_context(nc.sbuf_tensor(name, shape, dt))

            wq_hi = sb("wq_hi", [P, KD, 3 * D], F32R)
            wq_lo = sb("wq_lo", [P, KD, 3 * D], F32R)
            qT = sb("qT", [P, G, L])
            wo_hi = sb("wo_hi", [P, KD, D], F32R)
            wo_lo = sb("wo_lo", [P, KD, D], F32R)
            xT_hi = sb("xT_hi", [P, KD, BLK], F32R)
            xT_lo = sb("xT_lo", [P, KD, BLK], F32R)
            xq = sb("xq", [P, 2, D])
            xn = sb("xn", [P, TPB, D])
            k_hi = sb("k_hi", [P, 2, D], F32R)
            k_lo = sb("k_lo", [P, 2, D], F32R)
            vv_hi = sb("vv_hi", [P, 2, G, 2, 132], F32R)
            vv_lo = sb("vv_lo", [P, 2, G, 2, 132], F32R)
            work = sb("work", [P, 2, G, 132])
            xo = sb("xo", [P, 2, D])
            bk = sb("bk", [P, D])
            bv = sb("bv", [P, D])
            bo = sb("bo", [P, D])
            bq = sb("bq", [P, KD])
            ch = sb("ch", [P, KD, E])
            ch_hi = sb("ch_hi", [P, KD, E], F32R)
            ch_lo = sb("ch_lo", [P, KD, E], F32R)
            logit = sb("logit", [P, NT, E])
            prob = sb("prob", [P, NT, E])
            probE = sb("probE", [P, E, NT])
            probT = sb("probT", [P, 2, P])
            mark = sb("mark", [P, 2, P])
            stats = sb("stats", [P, 2, 6])
            mv = sb("mv", [P, 2, 2])
            var1 = sb("var1", [P, 2])
            std = sb("std", [P, 2])
            rstd = sb("rstd", [P, 2])
            newt = sb("newt", [P, 2])
            rden = sb("rden", [P, G, HPG])
            top = sb("top", [P, NT])
            thr = sb("thr", [P, 2], I32)
            cand = sb("cand", [P, 2], I32)
            hit = sb("hit", [P, 2], I32)
            cnt = sb("cnt", [P, 4])
            pre = sb("pre", [P, 4])
        kf = work[:, 0, :, :].rearrange("p g c -> p (g c)")[:, 0:D]
        vf = work[:, 1, :, :]
        sum_hi, sum_lo = vv_hi[:, 0, :, :, :], vv_lo[:, 0, :, :, :]

        def q_part(pair, par):
            return pair[:, 1, :, :, :].rearrange("p g t c -> p (g t c)")[:, par * D:(par + 1) * D].rearrange(
                "p (g c) -> p g c", g=G)

        with ExitStack() as late:
            def sb(name, shape, dt=F32):
                return late.enter_context(nc.sbuf_tensor(name, shape, dt))

            w1_raw = sb("w1_raw", [P, KD, F])
            w2_raw = sb("w2_raw", [P, KF, D])
            w1_hi = sb("w1_hi", [P, KD, F], F32R)
            w1_lo = sb("w1_lo", [P, KD, F], F32R)
            w2_hi = sb("w2_hi", [P, KF, D], F32R)
            w2_lo = sb("w2_lo", [P, KF, D], F32R)
            rows = sb("rows", [P, 2, TPB, ROW])
            xi_hi = sb("xi_hi", [P, KD, BLK], F32R)
            xi_lo = sb("xi_lo", [P, KD, BLK], F32R)
            h_hi = sb("h_hi", [P, KF, BLK], F32R)
            h_lo = sb("h_lo", [P, KF, BLK], F32R)
            hf = sb("hf", [P, 2, BLK])
            y = sb("y", [P, TPB, D])
            one_lo = sb("one_lo", [P, 2, 8, P], BF16)
            one_hi = sb("one_hi", [P, NT, 8], BF16)
            pay = sb("pay", [P, NT, 16], BF16)
            idx_f = sb("idx_f", [P, 8])
            idx_next = sb("idx_next", [P, B * SLOT_TILES], I32)
            idx = sb("idx", [P, B * SLOT_TILES], I32)

        con_in, wq_in, wo_in = sem("con_in"), sem("wq_in"), sem("wo_in")
        x_in, xn_ready = sem("x_in"), sem("xn_ready")
        xn_stored = [sem(f"xn_stored{s}") for s in range(2)]
        dve_steps = sem("dve_steps")
        prep_done, wsplit_hi = sem("prep_done"), sem("wsplit_hi")
        var_ready, std_ready = sem("var_ready"), sem("std_ready")
        tr_done, xT_hi_ready, xT_ready = sem("tr_done"), sem("xT_hi_ready"), sem("xT_ready")
        mm_done, lg_done, lg_read = sem("mm_done"), sem("lg_done"), sem("lg_read")
        k_read, v_read = sem("k_read"), sem("v_read")
        q_read = [sem(f"q_read{s}") for s in range(2)]
        k_hi_ready, k_ready, vv_ready = sem("k_hi_ready"), sem("k_ready"), sem("vv_ready")
        kv_zero, kv_done = sem("kv_zero"), sem("kv_done")
        sums_ready = sem("sums_ready")
        q_hi_ready, q_ready, ctx_done = sem("q_hi_ready"), sem("q_ready"), sem("ctx_done")
        sin_ready, o_raw, o_ready = sem("sin_ready"), sem("o_raw"), sem("o_ready")
        otr_done, oT_hi_ready, oT_ready = sem("otr_done"), sem("oT_hi_ready"), sem("oT_ready")
        out_done, res_ready, fin = sem("out_done"), sem("res_ready"), sem("fin")
        xo_in = [sem(f"xo_in{s}") for s in range(2)]
        out_stored = [sem(f"out_stored{s}") for s in range(2)]
        soft_sub, soft_exp, prob_ready, prob_stored = sem("soft_sub"), sem("soft_exp"), sem("prob_ready"), sem("prob_stored")
        route_dve, route_pe = sem("route_dve"), sem("route_pe")
        rank_out = sem("rank_out")
        w1_in, w2_in = sem("w1_in"), sem("w2_in")
        w1_hi_ready, w1_ready, w2_hi_ready, w2_ready = sem("w1_hi_ready"), sem("w1_ready"), sem("w2_hi_ready"), sem("w2_ready")
        rows_in = [sem(f"rows_in{s}") for s in range(2)]
        list_dve, list_pe, idx_ready, idx_copied = sem("list_dve"), sem("list_pe"), sem("idx_ready"), sem("idx_copied")
        gtr_done, xi_hi_ready, xi_ready = sem("gtr_done"), sem("xi_hi_ready"), sem("xi_ready")
        up_done, silu_done, h_ready = sem("up_done"), sem("silu_done"), sem("h_ready")
        down_done, y_ready = sem("down_done"), sem("y_ready")
        added = [sem(f"added{b}") for b in range(B)]

        block = ctx.enter_context(nc.Block())

        def first(t, n):
            return not isinstance(t, int) or t >= n

        def apart(eng):
            eng.nop(nofuse=True)

        def stage2_steps(eng, step):
            for t in range(2):
                step(t, t % 2)
            with eng.Fori(0, (NT - 4) // 2) as j:
                for s in range(2):
                    step(j * 2 + (2 + s), s)
            for t in range(NT - 2, NT + 2):
                step(t, t % 2)

        @block.sync
        def _(sp):
            sp.dma_start(con[:, :], consts).then_inc(con_in, 16)
            sp.dma_start(bit[:, :], bits).then_inc(con_in, 16)
            sp.dma_start(xq[:, :, :], xf[0:2 * P, :].rearrange("(t p) d -> p t d", p=P)).then_inc(x_in, 16)
            raw = qT[:, :, :].rearrange("p g l -> p (g l)")
            for k in range(KD):
                sp.dma_start(raw[:, k * 3 * D:(k + 1) * 3 * D], w_qkv[k * P:(k + 1) * P, :]).then_inc(wq_in, 16)
                sp.wait_ge(wq_in, 16 * (k + 1))
            sp.dma_start(raw[:, 3 * D * KD:3 * D * KD + KD * D].rearrange("p (k d) -> p k d", k=KD),
                         w_out.rearrange("(k p) d -> p k d", p=P)).then_inc(wo_in, 16)
            for n, dst in ((1, bk), (2, bv)):
                sp.dma_start(dst[:, :], b_qkv[n * D:(n + 1) * D].rearrange("(a d) -> a d", a=1).to_broadcast([P, D])
                             ).then_inc(con_in, 16)
            sp.dma_start(bo[:, :], b_out.rearrange("(a d) -> a d", a=1).to_broadcast([P, D])).then_inc(con_in, 16)
            with nc.allow_non_contiguous_dma("small transposed loads"):
                sp.dma_start(bq[:, :], b_qkv[0:D].rearrange("(m p) -> p m", p=P)).then_inc(con_in, 16)
                for k in range(KD):
                    sp.dma_start(ch[:, k, :], choice_w[:, k * P:(k + 1) * P].rearrange("e p -> p e")
                                 ).then_inc(con_in, 16)

            def store_normed(j, s):
                sp.wait_ge(xn_ready, j * TPB + (2 * s + 2))
                sp.dma_start(scratch[bass.ds(j * BLK + 2 * s * P, 2 * P), 0:D].rearrange("(t p) d -> p t d", p=P),
                             xn[:, 2 * s:2 * s + 2, :]).then_inc(xn_stored[s], 16)

            def load_x(row):
                sp.dma_start(xq[:, :, :], xf[bass.ds(row, 2 * P), :].rearrange("(t p) d -> p t d", p=P)
                             ).then_inc(x_in, 16)

            store_normed(0, 0)
            load_x(2 * P)
            store_normed(0, 1)
            with sp.Fori(0, B) as b:
                with sp.Fori(0, NBLK) as i:
                    nxt = b * NBLK + i + 1
                    src = (nxt % (B * NBLK)) * BLK
                    for s in range(2):
                        sp.wait_ge(xn_ready, nxt * TPB + 2 * s)
                        load_x(src + 2 * s * P)
                        sp.wait_ge(xn_ready, nxt * TPB + (2 * s + 2))
                        sp.dma_start(scratch[bass.ds(src + 2 * s * P, 2 * P), 0:D].rearrange("(t p) d -> p t d", p=P),
                                     xn[:, 2 * s:2 * s + 2, :]).then_inc(xn_stored[s], 16)

                def load_res(t, par):
                    sp.dma_start(xo[:, par, :], xf[bass.ds(b * L + t * P, P), :]).then_inc(xo_in[par], 16)

                for t in range(2):
                    sp.wait_ge(out_stored[t], b * (NT // 2) * 16)
                    load_res(t, t)
                sp.wait_ge(prob_ready, b + 1)
                sp.dma_start(scratch[bass.ds(b * L, L), D:ROW].rearrange("(t p) e -> p t e", p=P),
                             prob[:, :, :]).then_inc(prob_stored, 16)

                def store_out(t, par):
                    sp.wait_ge(fin, b * NT + t + 1)
                    sp.dma_start(of[bass.ds(b * L + t * P, P), :], xo[:, par, :]).then_inc(out_stored[par], 16)

                with sp.Fori(0, NT // 2 - 1) as j:
                    for par in range(2):
                        store_out(j * 2 + par, par)
                        sp.wait_ge(out_stored[par], (b * (NT // 2) + j + 1) * 16)
                        load_res(j * 2 + (2 + par), par)
                for par in range(2):
                    store_out(NT - 2 + par, par)

            def load_w1(e):
                sp.dma_start(w1_raw[:, :, :], w1[bass.ds(e, 1), :, :].rearrange("e (k p) f -> p (e k) f", p=P)
                             ).then_inc(w1_in, 16)

            def load_w2(e):
                sp.dma_start(w2_raw[:, :, :], w2[bass.ds(e, 1), :, :].rearrange("e (k p) d -> p (e k) d", p=P)
                             ).then_inc(w2_in, 16)

            sp.wait_ge(route_pe, B * ROUTE)
            load_w1(0)
            load_w2(0)
            with sp.Fori(0, E) as e:
                nxt_e = (e + 1) % E
                sp.wait_ge(w1_ready, (e + 1) * KF)
                load_w1(nxt_e)
                sp.wait_ge(w2_ready, (e + 1) * KF)
                load_w2(nxt_e)
            sp.wait_ge(w1_in, 16 * (E + 1))
            sp.wait_ge(w2_in, 16 * (E + 1))
            for s in range(2):
                sp.wait_ge(xn_stored[s], 16 * (B * NBLK + 1))
                sp.wait_ge(out_stored[s], 16 * B * NT // 2)
            sp.wait_ge(prob_stored, 16 * B)
            for b in range(B):
                sp.wait_ge(added[b], 16 * E * SLOT_TILES)

        @block.gpsimd
        def _(pool):
            pool.wait_ge(con_in, CON_LOADS * 16)
            with pool.Fori(0, B) as b:
                with pool.Fori(0, NT // 2) as j:
                    for par in range(2):
                        n = b * NT + j * 2 + par
                        pool.wait_ge(xo_in[par], (b * (NT // 2) + j + 1) * 16)
                        nc.gpsimd.tensor_tensor(xo[:, par, :], xo[:, par, :], bo[:, :], ALU.add).then_inc(res_ready, 1)

            def gather(table, col, buf, tt):
                nc.gpsimd.indirect_dma_start(rows[:, buf, tt, :], None, scratch[:, :],
                                             bass.IndirectOffsetOnAxis(ap=table[:, col:col + 1], axis=0)
                                             ).then_inc(rows_in[buf], 16)

            def copy_list():
                nc.gpsimd.tensor_copy(idx[:, :], idx_next[:, :]).then_inc(idx_copied, 1)

            for s in range(2):
                pool.wait_ge(xn_stored[s], 16 * (B * NBLK + 1))
                pool.wait_ge(out_stored[s], 16 * B * NT // 2)
            pool.wait_ge(prob_stored, 16 * B)
            pool.wait_ge(idx_ready, B)
            for tt in range(TPB):
                gather(idx_next, tt, 0, tt)
            copy_list()
            with pool.Fori(0, E) as e:
                for u in range(UNITS):
                    b, half = u // HALVES, u % HALVES
                    pool.wait_ge(y_ready, e * (UNITS * TPB) + u * TPB)
                    if u == UNITS - 1:
                        pool.wait_ge(idx_ready, e * B + 2 * B)
                    elif u == 0:
                        pool.wait_ge(idx_copied, e + 1)
                    apart(pool)
                    for tt in range(TPB):
                        if u == UNITS - 1:
                            gather(idx_next, tt, 0, tt)
                        else:
                            gather(idx, (u + 1) * TPB + tt, (u + 1) % 2, tt)
                    if half == 0:
                        pool.wait_ge(added[b], e * (16 * SLOT_TILES))
                    for tt in range(TPB):
                        pool.wait_ge(y_ready, e * (UNITS * TPB) + (u * TPB + tt + 1))
                        apart(pool)
                        nc.gpsimd.indirect_dma_start(
                            of[:, :], bass.IndirectOffsetOnAxis(ap=idx[:, u * TPB + tt:u * TPB + tt + 1], axis=0),
                            y[:, tt, :], None, compute_op=ALU.add).then_inc(added[b], 16)
                for b in range(B):
                    pool.wait_ge(added[b], (e + 1) * (16 * SLOT_TILES))
                pool.wait_ge(rows_in[0], e * (64 * UNITS // 2) + 64 * (UNITS // 2 + 1))
                apart(pool)
                copy_list()
            pool.wait_ge(rows_in[0], 64 * (E * UNITS // 2 + 1))

        @block.scalar
        def _(act):
            raw = qT[:, :, :].rearrange("p g l -> p (g l)")
            for k in range(KD):
                act.wait_ge(wq_in, 16 * (k + 1))
                nc.scalar.copy(wq_hi[:, k, :], raw[:, k * 3 * D:(k + 1) * 3 * D]).then_inc(wsplit_hi, 1)
            act.wait_ge(wo_in, 16)
            nc.scalar.copy(wo_hi[:, :, :], raw[:, 3 * D * KD:3 * D * KD + KD * D].rearrange("p (k d) -> p k d", k=KD)
                           ).then_inc(wsplit_hi, 1)
            act.wait_ge(con_in, CON_LOADS * 16)
            nc.scalar.copy(ch_hi[:, :, :], ch[:, :, :]).then_inc(wsplit_hi, 1)

            def sqrt(j, s):
                act.wait_ge(var_ready, j * 2 + s + 1)
                nc.scalar.activation(std[:, :], var1[:, :], ACT.Sqrt).then_inc(std_ready, 1)

            def turned_hi(j, t, matmuls):
                act.wait_ge(tr_done, j * TPB + t + 1)
                if matmuls is not None:
                    act.wait_ge(mm_done, matmuls)
                nc.scalar.copy(xT_hi[:, :, t * P:(t + 1) * P],
                               ps[:, 6 + t % 2, :].rearrange("p (k c) -> p k c", k=KD)).then_inc(xT_hi_ready, 1)

            sqrt(0, 0)
            sqrt(0, 1)
            turned_hi(0, 0, None)
            turned_hi(0, 1, None)
            act.wait_ge(prep_done, 1)
            with act.Fori(0, B) as b:
                with act.Fori(0, NBLK) as i:
                    n = b * NBLK + i
                    turned_hi(n, 2, n * 12)
                    turned_hi(n, 3, n * 12)
                    sqrt(n + 1, 0)
                    for t in range(TPB):
                        act.wait_ge(k_read, n * TPB + t + 1)
                        act.wait_ge(kv_done, n * TPB + max(t - 1, 0))
                        nc.scalar.activation(k_hi[:, t % 2, :], kf, ACT.Relu).then_inc(k_hi_ready, 1)
                        act.wait_ge(mm_done, n * 12 + 2 * t + 2)
                        act.wait_ge(vv_ready, n * TPB + t)
                        nc.scalar.copy(vf[:, :, 0:P], ps[:, 5, :].rearrange("p (g c) -> p g c", g=G)
                                       ).then_inc(v_read, 1)
                        if t == 0:
                            sqrt(n + 1, 1)

                    def q_out(m):
                        act.wait_ge(mm_done, n * 12 + 9 + m)
                        nc.scalar.activation(qT[:, m, bass.ds(i * BLK, BLK)], ps[:, 4 + m % 2, :], ACT.Relu,
                                             bias=bq[:, m:m + 1]).then_inc(q_read[m % 2], 1)

                    for m in range(3):
                        q_out(m)
                    turned_hi(n + 1, 0, n * 12 + 12)
                    turned_hi(n + 1, 1, None)
                    q_out(3)

                def q_hi(t, par):
                    if first(t, 2):
                        act.wait_ge(ctx_done, b * NT + t - 1)
                    nc.scalar.copy(q_part(vv_hi, par), qT[:, :, bass.ds(t * P, P)]).then_inc(q_hi_ready, 1)

                act.wait_ge(kv_done, (b + 1) * NT)
                q_hi(0, 0)

                def step(t, par):
                    if not isinstance(t, int) or t < NT - 1:
                        q_hi(t + 1, 1 - par)
                    if not isinstance(t, int) or t < NT:
                        act.wait_ge(ctx_done, b * NT + t + 1)
                        act.wait_ge(o_raw, b * NT + t)
                        nc.scalar.activation(work[:, 0, :, :], ps[:, 0:4, 132:264], ACT.Copy,
                                             scale=con[:, bass.ds(C_SIN + t, 1)]).then_inc(sin_ready, 1)
                    if isinstance(t, int) and t == 0:
                        act.wait_ge(soft_sub, b + 1)
                        nc.scalar.activation(logit[:, :, :], logit[:, :, :], ACT.Exp).then_inc(soft_exp, 1)
                    if first(t, 1) and not (isinstance(t, int) and t > NT):
                        act.wait_ge(otr_done, b * NT + t)
                        if first(t, 3):
                            act.wait_ge(out_done, b * NT + t - 2)
                        nc.scalar.copy(k_hi[:, 1 - par, :], ps[:, 6, :]).then_inc(oT_hi_ready, 1)

                stage2_steps(act, step)

            def w1_high(e, m):
                sl = slice(m * P, (m + 1) * P)
                nc.scalar.copy(w1_hi[:, :, sl], w1_raw[:, :, sl]).then_inc(w1_hi_ready, 1)

            def rows_hi(unit, tt):
                act.wait_ge(gtr_done, unit * TPB + tt + 1)
                nc.scalar.copy(xi_hi[:, :, tt * P:(tt + 1) * P],
                               ps[:, 6 + tt % 2, :].rearrange("p (k c) -> p k c", k=KD)).then_inc(xi_hi_ready, 1)

            act.wait_ge(w1_in, 16)
            for m in range(KF):
                w1_high(0, m)
            for tt in range(TPB):
                rows_hi(0, tt)
            with act.Fori(0, E) as e:
                for u in range(UNITS):
                    n = e * UNITS + u
                    b, half = u // HALVES, u % HALVES
                    for m in range(KF):
                        act.wait_ge(up_done, n * KF + m + 1)
                        act.wait_ge(h_ready, n * KF + max(m - 1, 0))
                        nc.scalar.activation(hf[:, m % 2, :], ps[:, m % 2, :], ACT.Silu).then_inc(silu_done, 1)
                        if u == 0:
                            if m == 0:
                                act.wait_ge(w2_in, (e + 1) * 16)
                                act.wait_ge(down_done, n * TPB)
                            nc.scalar.copy(w2_hi[:, m, :], w2_raw[:, m, :]).then_inc(w2_hi_ready, 1)
                    act.wait_ge(added[(u + UNITS - 1) % UNITS // HALVES],
                                e * (16 * SLOT_TILES) + [0, 4, 8, 4][u] * 16)
                    for tt in range(TPB):
                        act.wait_ge(down_done, n * TPB + tt + 1)
                        apart(act)
                        nc.scalar.activation(y[:, tt, :], ps[:, 2 + tt % 2, :], ACT.Copy,
                                             scale=rows[:, u % 2, tt, bass.ds(D + e, 1)]).then_inc(y_ready, 1)
                        rows_hi(n + 1, tt)
                        if u == UNITS - 1:
                            if tt == 0:
                                act.wait_ge(w1_in, e * 16 + 32)
                            for m in (2 * tt, 2 * tt + 1):
                                w1_high(e, m)

        @block.vector
        def _(dve):
            me = Steps(dve, dve_steps)
            raw = qT[:, :, :].rearrange("p g l -> p (g l)")

            def norm_half(j, s, reuse):
                dve.wait_ge(x_in, (j * 2 + s + 1) * 16)
                for tt in range(2):
                    me.did(nc.vector.bn_stats(stats[:, tt, :], xq[:, tt, :]))
                me.wait()
                apart(dve)
                for tt in range(2):
                    me.did(nc.vector.bn_aggr(mv[:, tt, :], stats[:, tt, :]))
                me.wait()
                nc.vector.tensor_scalar(var1[:, :], mv[:, :, 1], LN_EPS, None, ALU.add).then_inc(var_ready, 1)
                dve.wait_ge(std_ready, j * 2 + s + 1)
                me.did(nc.vector.reciprocal(rstd[:, :], std[:, :]))
                me.wait()
                me.did(nc.vector.tensor_tensor(newt[:, :], rstd[:, :], rstd[:, :], ALU.mult))
                me.wait()
                me.did(nc.vector.tensor_tensor(newt[:, :], newt[:, :], var1[:, :], ALU.mult))
                me.wait()
                me.did(nc.vector.tensor_scalar(newt[:, :], newt[:, :], -0.5, 1.5, ALU.mult, ALU.add))
                me.wait()
                me.did(nc.vector.tensor_tensor(rstd[:, :], rstd[:, :], newt[:, :], ALU.mult))
                me.wait()
                if reuse:
                    dve.wait_ge(xn_stored[s], j * 16)
                    dve.wait_ge(tr_done, j * TPB - 2 + 2 * s)
                for tt in range(2):
                    nc.vector.tensor_scalar(xn[:, 2 * s + tt, :], xq[:, tt, :], mv[:, tt, 0:1], rstd[:, tt:tt + 1],
                                            ALU.subtract, ALU.mult).then_inc(xn_ready, 1)

            def turned_lo(j, t):
                dve.wait_ge(xT_hi_ready, j * TPB + t + 1)
                sl = slice(t * P, (t + 1) * P)
                nc.vector.tensor_tensor(xT_lo[:, :, sl], ps[:, 6 + t % 2, :].rearrange("p (k c) -> p k c", k=KD),
                                        xT_hi[:, :, sl].bitcast(F32), ALU.subtract).then_inc(xT_ready, 1)

            dve.wait_ge(con_in, CON_LOADS * 16)
            me.did(nc.vector.tensor_copy(iota_bf[:, :], con[:, C_IOTA:C_COS]))
            norm_half(0, 0, False)
            norm_half(0, 1, False)
            for k in range(KD):
                dve.wait_ge(wsplit_hi, k + 1)
                nc.vector.tensor_tensor(wq_lo[:, k, :], raw[:, k * 3 * D:(k + 1) * 3 * D], wq_hi[:, k, :].bitcast(F32),
                                        ALU.subtract)
            dve.wait_ge(wsplit_hi, KD + 1)
            nc.vector.tensor_tensor(wo_lo[:, :, :].rearrange("p k d -> p (k d)"),
                                    raw[:, 3 * D * KD:3 * D * KD + KD * D],
                                    wo_hi[:, :, :].rearrange("p k d -> p (k d)").bitcast(F32), ALU.subtract)
            dve.wait_ge(wsplit_hi, KD + 2)
            nc.vector.tensor_tensor(ch_lo[:, :, :], ch[:, :, :], ch_hi[:, :, :].bitcast(F32),
                                    ALU.subtract).then_inc(prep_done, 1)
            nc.vector.memset(rank_lo[:, :, :, :], -1.0)
            nc.vector.memset(zero[:, :], 0.0)
            nc.vector.memset(rank_hi[:, :, :, :], -1.0).then_inc(prep_done, 1)
            turned_lo(0, 0)
            turned_lo(0, 1)

            N_BLOCK, N_PAIR, N_BATCH, N_EXPERT = 2 * 9 + 2 * TPB, 10, 411, 40

            with dve.Fori(0, B) as b:
                me.enter(b, N_BATCH)
                me.did(nc.vector.memset(vf[:, :, P:P + 1], 1.0))
                me.did(nc.vector.memset(vf[:, :, P + 1:VW], 0.0))
                me.wait()
                apart(dve)
                with dve.Fori(0, NBLK) as i:
                    me.enter(i, N_BLOCK)
                    n = b * NBLK + i
                    turned_lo(n, 2)
                    turned_lo(n, 3)
                    norm_half(n + 1, 0, True)
                    for t in range(TPB):
                        par = t % 2
                        dve.wait_ge(mm_done, n * 12 + 2 * t + 1)
                        nc.vector.tensor_tensor(kf, ps[:, 4, :], bk[:, :], ALU.add).then_inc(k_read, 1)
                        dve.wait_ge(k_hi_ready, n * TPB + t + 1)
                        nc.vector.scalar_tensor_tensor(k_lo[:, par, :], kf, 0.0, k_hi[:, par, :].bitcast(F32),
                                                       ALU.max, ALU.subtract).then_inc(k_ready, 1)
                        dve.wait_ge(v_read, n * TPB + t + 1)
                        v = vf[:, :, 0:VW]
                        for trig, c in ((0, C_COS), (1, C_SIN)):
                            me.did(nc.vector.tensor_scalar(vv_hi[:, par, :, trig, 0:VW], v,
                                                           con[:, bass.ds(c + i * TPB + t, 1)], None, ALU.mult))
                        me.wait()
                        for trig, c in ((0, C_COS), (1, C_SIN)):
                            last = nc.vector.scalar_tensor_tensor(
                                vv_lo[:, par, :, trig, 0:VW], v, con[:, bass.ds(c + i * TPB + t, 1)],
                                vv_hi[:, par, :, trig, 0:VW].bitcast(F32), ALU.mult, ALU.subtract)
                        last.then_inc(vv_ready, 1)
                        if t == 0:
                            norm_half(n + 1, 1, True)
                    dve.wait_ge(lg_done, n + 1)
                    nc.vector.tensor_copy(logit[:, bass.ds(i * TPB, TPB), :],
                                          ps[:, 7, 0:TPB * E].rearrange("p (t e) -> p t e", e=E)).then_inc(lg_read, 1)
                    turned_lo(n + 1, 0)
                    turned_lo(n + 1, 1)
                    me.leave(NBLK)

                dve.wait_ge(kv_done, (b + 1) * NT)
                sums = work[:, :, :, :].rearrange("p a g c -> p (a g c)").rearrange("p (g t c) -> p g t c", g=G, t=2)
                for g in range(G):
                    for trig in range(2):
                        at = trig * VW
                        me.did(nc.vector.scalar_tensor_tensor(
                            sums[:, g, trig, 0:P], bv[:, g * P:(g + 1) * P], ps[:, g, at + P:at + P + 1],
                            ps[:, g, at:at + P], ALU.mult, ALU.add))
                        me.did(nc.vector.tensor_scalar(sums[:, g, trig, P:P + HPG], con[:, C_HEAD:C_END],
                                                       ps[:, g, at + P:at + P + 1], None, ALU.mult))
                me.wait()
                for g in range(G):
                    for trig in range(2):
                        me.did(nc.vector.tensor_tensor(sums[:, g, trig, 0:P], sums[:, g, trig, 0:P], same_block,
                                                       ALU.mult))
                me.wait()
                me.did(nc.vector.tensor_copy(sum_hi, sums))
                me.wait()
                nc.vector.tensor_tensor(sum_lo, sums, sum_hi.bitcast(F32), ALU.subtract).then_inc(sums_ready, 1)

                def q_lo(t, par):
                    dve.wait_ge(q_hi_ready, b * NT + t + 1)
                    nc.vector.tensor_tensor(q_part(vv_lo, par), qT[:, :, bass.ds(t * P, P)],
                                            q_part(vv_hi, par).bitcast(F32), ALU.subtract).then_inc(q_ready, 1)

                q_lo(0, 0)

                def softmax():
                    me.did(nc.vector.tensor_reduce(top[:, :], logit[:, :, :], AX.X, ALU.max))
                    me.wait()
                    nc.vector.tensor_tensor(logit[:, :, :], logit[:, :, :],
                                            top[:, :].rearrange("p (t e) -> p t e", e=1).to_broadcast([P, NT, E]),
                                            ALU.subtract).then_inc(soft_sub, 1)
                    dve.wait_ge(soft_exp, b + 1)
                    me.did(nc.vector.tensor_reduce(top[:, :], logit[:, :, :], AX.X, ALU.add))
                    me.wait()
                    me.did(nc.vector.reciprocal(top[:, :], top[:, :]))
                    me.wait()
                    dve.wait_ge(prob_stored, b * 16)
                    nc.vector.tensor_tensor(prob[:, :, :], logit[:, :, :],
                                            top[:, :].rearrange("p (t e) -> p t e", e=1).to_broadcast([P, NT, E]),
                                            ALU.mult).then_inc(prob_ready, 1)
                    dve.wait_ge(prob_ready, b + 1)
                    nc.vector.tensor_copy(probE[:, :, :].rearrange("p e t -> p t e"), prob[:, :, :]
                                          ).then_inc(route_dve, 1)

                def search_start():
                    dve.wait_ge(route_pe, b * ROUTE + 1)
                    me.did(nc.vector.tensor_copy(probT[:, :, :].rearrange("p h c -> p (h c)"), ps[:, 7, 0:2 * P]))
                    me.did(nc.vector.memset(thr[:, :], 0))
                    me.wait()

                def count(s):
                    me.did(nc.vector.tensor_tensor(cand[:, :], thr[:, :], bit[:, bass.ds(s, 1)].to_broadcast([P, 2]),
                                                   ALU.bitwise_or))
                    me.wait()
                    for h in range(2):
                        last = nc.vector.tensor_scalar(mark[:, h, :], probT[:, h, :], cand[:, h:h + 1].bitcast(F32),
                                                       None, ALU.is_ge, ALU.add, accum_out=cnt[:, h:h + 1])
                    last.then_inc(route_dve, 1)

                def settle(s):
                    dve.wait_ge(route_pe, b * ROUTE + s + 2)
                    me.did(nc.vector.tensor_scalar(hit[:, :], ps[:, 7, 0:2], float(CAP) - 0.5, None, ALU.is_ge))
                    me.wait()
                    apart(dve)
                    me.did(nc.vector.copy_predicated(thr[:, :], hit[:, :], cand[:, :]))
                    me.wait()

                def step(t, par):
                    if first(t, 2) and not (isinstance(t, int) and t >= NT):
                        settle(t - 2)
                        if not isinstance(t, int) or t < NT - 1:
                            count(t - 1)
                    if not isinstance(t, int) or t < NT - 1:
                        q_lo(t + 1, 1 - par)
                    if not isinstance(t, int) or t < NT:
                        o = work[:, 1, :, :]
                        dve.wait_ge(sin_ready, b * NT + t + 1)
                        dve.wait_ge(otr_done, b * NT + t)
                        nc.vector.scalar_tensor_tensor(
                            o, ps[:, 0:4, 0:132], con[:, bass.ds(C_COS + t, 1)], work[:, 0, :, :],
                            ALU.mult, ALU.add).then_inc(o_raw, 1)
                        dve.wait_ge(o_raw, b * NT + t + 1)
                        me.did(nc.vector.tensor_scalar(rden[:, :, :], o[:, :, P:P + HPG], NORM_EPS, None, ALU.add))
                        me.wait()
                        me.did(nc.vector.reciprocal(rden[:, :, :], rden[:, :, :]))
                        me.wait()
                        o4 = o[:, :, 0:P].rearrange("p g (h c) -> p g h c", h=HPG)
                        r4 = rden[:, :, :].rearrange("p g (h c) -> p g h c", c=1).to_broadcast([P, G, HPG, HD])
                        nc.vector.tensor_tensor(o4, o4, r4, ALU.mult).then_inc(o_ready, 1)
                    if isinstance(t, int) and t == 0:
                        softmax()
                    if isinstance(t, int) and t == 1:
                        search_start()
                        count(0)
                    if first(t, 1) and not (isinstance(t, int) and t > NT):
                        dve.wait_ge(oT_hi_ready, b * NT + t)
                        nc.vector.tensor_tensor(k_lo[:, 1 - par, :], ps[:, 6, :], k_hi[:, 1 - par, :].bitcast(F32),
                                                ALU.subtract).then_inc(oT_ready, 1)
                    if first(t, 2):
                        dve.wait_ge(out_done, b * NT + t - 1)
                        dve.wait_ge(res_ready, b * NT + t - 1)
                        nc.vector.tensor_tensor(xo[:, par, :], ps[:, 4 + par, :], xo[:, par, :],
                                                ALU.add).then_inc(fin, 1)

                def dve_steps2():
                    for t in range(2):
                        step(t, t % 2)
                    with dve.Fori(0, (NT - 4) // 2) as j:
                        me.enter(j, N_PAIR)
                        for s in range(2):
                            step(j * 2 + (2 + s), s)
                        me.leave((NT - 4) // 2)
                    for t in range(NT - 2, NT + 2):
                        step(t, t % 2)

                dve_steps2()

                above, equal = logit[:, :, :].rearrange("p t e -> p (t e)"), probE[:, :, :].rearrange("p e t -> p (e t)")
                above, equal = (a.rearrange("p (h c) -> p h c", h=2) for a in (above, equal))
                for h in range(2):
                    t_h = thr[:, h:h + 1].bitcast(F32)
                    me.did(nc.vector.tensor_scalar(above[:, h, :], probT[:, h, :], t_h, None, ALU.is_gt, ALU.add,
                                                   accum_out=cnt[:, h:h + 1]))
                    last = nc.vector.tensor_scalar(equal[:, h, :], probT[:, h, :], t_h, None, ALU.is_equal, ALU.add,
                                                   accum_out=cnt[:, 2 + h:3 + h])
                last.then_inc(route_dve, 1)
                dve.wait_ge(route_pe, b * ROUTE + BITS + 2)
                me.did(nc.vector.tensor_scalar(pre[:, 0:2], ps[:, 7, 0:2], -1.0, float(CAP), ALU.mult, ALU.add))
                me.did(nc.vector.tensor_copy(pre[:, 2:4], ps[:, 7, 4:6]))
                me.wait()
                for h in range(2):
                    me.did(nc.vector.tensor_tensor_scan(mark[:, h, :], equal[:, h, :], equal[:, h, :],
                                                        pre[:, 2 + h:3 + h], ALU.add, ALU.max))
                me.wait()
                for h in range(2):
                    me.did(nc.vector.scalar_tensor_tensor(mark[:, h, :], mark[:, h, :], pre[:, h:h + 1],
                                                          equal[:, h, :], ALU.is_le, ALU.mult))
                me.wait()
                me.did(nc.vector.tensor_tensor(above, above, mark[:, :, :], ALU.add))
                me.wait()
                nc.vector.tensor_reduce(cnt[:, 0:2], above, AX.X, ALU.add).then_inc(route_dve, 1)
                dve.wait_ge(route_pe, b * ROUTE + BITS + 3)
                me.did(nc.vector.tensor_copy(pre[:, 2:4], ps[:, 7, 0:2]))
                me.wait()
                for h in range(2):
                    me.did(nc.vector.tensor_tensor_scan(mark[:, h, :], above[:, h, :], above[:, h, :],
                                                        pre[:, 2 + h:3 + h], ALU.add, ALU.max))
                me.wait()
                me.did(nc.vector.tensor_tensor(mark[:, :, :], mark[:, :, :], above, ALU.mult))
                me.wait()
                nc.vector.tensor_scalar(mark[:, :, :], mark[:, :, :], -1.0, None, ALU.add).then_inc(route_dve, 1)
                dve.wait_ge(route_pe, b * ROUTE + BITS + 4)
                rank_i = probT[:, :, :].rearrange("p h c -> p (h c)").bitcast(I32)
                part_i = mark[:, :, :].rearrange("p h c -> p (h c)").bitcast(I32)
                nc.vector.tensor_copy(rank_i, ps[:, 7, 0:2 * P]).then_inc(rank_out, 1)
                dve.wait_ge(rank_out, b + 1)
                for op, by, dst in ((ALU.bitwise_and, P - 1, rank_lo), (ALU.arith_shift_right, 7, rank_hi)):
                    me.did(nc.vector.tensor_scalar(part_i, rank_i, by, None, op))
                    me.wait()
                    me.did(nc.vector.tensor_copy(dst[:, bass.ds(b, 1), 0:E, :].rearrange("p b e t -> p (b e t)"),
                                                 part_i))
                    me.wait()
                me.leave(B)

            def list_head(e, b, turn):
                r = rank_hi[:, b, bass.ds(e, 1), :].rearrange("p e t -> p t e").to_broadcast([P, NT, 8])
                me.did(nc.vector.tensor_tensor(
                    one_hi[:, :, :], r,
                    con[:, C_EIGHT:C_TILE].rearrange("p (a c) -> p a c", a=1).to_broadcast([P, NT, 8]), ALU.is_equal))
                me.wait()
                dve.wait_ge(list_pe, turn * 4)
                me.did(nc.vector.tensor_tensor(
                    pay[:, :, 0:8], one_hi[:, :, :],
                    con[:, C_TILE:C_PCOL].rearrange("p (t a) -> p t a", a=1).to_broadcast([P, NT, 8]), ALU.mult))
                me.did(nc.vector.tensor_scalar(pay[:, :, 8:16], one_hi[:, :, :], con[:, C_PCOL:C_HEAD], None,
                                               ALU.mult))

            def list_part(e, b, turn, c):
                if c >= 2:
                    dve.wait_ge(list_pe, turn * 4 + c - 1)
                r = rank_lo[:, b, bass.ds(e, 1), c * 8:(c + 1) * 8].rearrange("p e t -> p t e").to_broadcast([P, 8, P])
                nc.vector.tensor_tensor(
                    one_lo[:, c % 2, :, :], r,
                    iota_bf[:, :].rearrange("p (a c) -> p a c", a=1).to_broadcast([P, 8, P]), ALU.is_equal
                ).then_inc(list_dve, 1)

            def list_tail(b, turn, copies):
                dve.wait_ge(list_pe, turn * 4 + 4)
                me.did(nc.vector.tensor_scalar(idx_f[:, :], ps[:, 4, 0:8], float(P), float(b * L), ALU.mult, ALU.add))
                me.wait()
                if copies is not None:
                    dve.wait_ge(idx_copied, copies)
                nc.vector.tensor_tensor(idx_next[:, b * SLOT_TILES:(b + 1) * SLOT_TILES], ps[:, 4, 8:16], idx_f[:, :],
                                        ALU.add).then_inc(idx_ready, 1)

            def w1_low(m, ready):
                dve.wait_ge(w1_hi_ready, ready)
                sl = slice(m * P, (m + 1) * P)
                nc.vector.tensor_tensor(w1_lo[:, :, sl], w1_raw[:, :, sl], w1_hi[:, :, sl].bitcast(F32),
                                        ALU.subtract).then_inc(w1_ready, 1)

            def rows_lo(unit, tt):
                dve.wait_ge(xi_hi_ready, unit * TPB + tt + 1)
                sl = slice(tt * P, (tt + 1) * P)
                nc.vector.tensor_tensor(xi_lo[:, :, sl], ps[:, 6 + tt % 2, :].rearrange("p (k c) -> p k c", k=KD),
                                        xi_hi[:, :, sl].bitcast(F32), ALU.subtract).then_inc(xi_ready, 1)

            for s in range(2):
                dve.wait_ge(out_stored[s], 16 * B * NT // 2)
                dve.wait_ge(xn_stored[s], 16 * (B * NBLK + 1))
            for b in range(B):
                list_head(0, b, b)
                for c in range(4):
                    list_part(0, b, b, c)
                list_tail(b, b, None)
            for m in range(KF):
                w1_low(m, m + 1)
            for tt in range(TPB):
                rows_lo(0, tt)
            with dve.Fori(0, E) as e:
                me.enter(e, N_EXPERT)
                for u in range(UNITS):
                    n = e * UNITS + u
                    for m in range(KF):
                        dve.wait_ge(silu_done, n * KF + m + 1)
                        if m == 0:
                            dve.wait_ge(down_done, n * TPB)
                        me.did(nc.vector.tensor_copy(h_hi[:, m, :], hf[:, m % 2, :]))
                        me.wait()
                        nc.vector.tensor_tensor(h_lo[:, m, :], hf[:, m % 2, :], h_hi[:, m, :].bitcast(F32),
                                                ALU.subtract).then_inc(h_ready, 1)
                        if u == 0:
                            dve.wait_ge(w2_hi_ready, e * KF + m + 1)
                            nc.vector.tensor_tensor(w2_lo[:, m, :], w2_raw[:, m, :], w2_hi[:, m, :].bitcast(F32),
                                                    ALU.subtract).then_inc(w2_ready, 1)
                    turn = e * B + (B + u)
                    if u < B:
                        list_head(e + 1, u, turn)
                    for tt in range(TPB):
                        if u < B:
                            list_part(e + 1, u, turn, tt)
                        rows_lo(n + 1, tt)
                        if u == UNITS - 1:
                            for m in (2 * tt, 2 * tt + 1):
                                w1_low(m, e * KF + (KF + m + 1))
                    if u < B:
                        list_tail(u, turn, e + 1)
                me.leave(E)

        @block.tensor
        def _(pe):
            def product(dst, lhs, rhs, start, stop):
                (a_hi, a_lo), (b_hi, b_lo) = lhs, rhs
                nc.tensor.matmul(dst, a_hi, b_hi, start=start, stop=False, skip_group_check=True)
                nc.tensor.matmul(dst, a_hi, b_lo, start=False, stop=False, skip_group_check=True)
                return nc.tensor.matmul(dst, a_lo, b_hi, start=False, stop=stop, skip_group_check=True)

            def pair(ab, *where):
                return tuple(a[where] for a in ab)

            xT, wq, wo, chs = (xT_hi, xT_lo), (wq_hi, wq_lo), (wo_hi, wo_lo), (ch_hi, ch_lo)
            al = slice(None)

            def turn_x(t, ready):
                pe.wait_ge(xn_ready, ready)
                for k in range(KD):
                    last = nc.tensor.transpose(ps[:, 6 + t % 2, k * P:(k + 1) * P], xn[:, t, k * P:(k + 1) * P], ident)
                last.then_inc(tr_done, 1)

            pe.wait_ge(con_in, CON_LOADS * 16)
            turn_x(0, 1)
            turn_x(1, 2)
            pe.wait_ge(prep_done, 2)
            with pe.Fori(0, B) as b:
                for g in range(G):
                    nc.tensor.matmul(ps[:, g, 0:2 * VW], iota_bf[:, :], zero[:, :], start=True, stop=False,
                                     skip_group_check=True)
                with pe.Fori(0, NBLK) as i:
                    n = b * NBLK + i
                    for t in (2, 3):
                        pe.wait_ge(xT_ready, n * TPB + t - 1)
                        turn_x(t, n * TPB + t + 1)

                    def kv(t):
                        par = t % 2
                        pe.wait_ge(k_ready, n * TPB + t + 1)
                        pe.wait_ge(vv_ready, n * TPB + t + 1)
                        for g in range(G):
                            cols = slice(g * P, (g + 1) * P)
                            last = product(ps[:, g, 0:2 * VW].rearrange("p (a c) -> p a c", a=2),
                                           pair((k_hi, k_lo), al, par, cols),
                                           pair((vv_hi, vv_lo), al, par, g, al, slice(0, VW)), False, False)
                        last.then_inc(kv_done, 1)

                    for t in range(TPB):
                        tok = slice(t * P, (t + 1) * P)
                        pe.wait_ge(xT_ready, n * TPB + t + 1)
                        if t == 0:
                            pe.wait_ge(q_read[0], n * 2)
                        else:
                            pe.wait_ge(k_read, n * TPB + t)
                        for k in range(KD):
                            last = product(ps[:, 4, :], pair(xT, al, k, tok), pair(wq, al, k, slice(D, 2 * D)),
                                           k == 0, k == KD - 1)
                        last.then_inc(mm_done, 1)
                        if t == 0:
                            pe.wait_ge(q_read[1], n * 2)
                        else:
                            pe.wait_ge(v_read, n * TPB + t)
                        for k in range(KD):
                            last = product(ps[:, 5, :], pair(xT, al, k, tok), pair(wq, al, k, slice(2 * D, 3 * D)),
                                           k == 0, k == KD - 1)
                        last.then_inc(mm_done, 1)
                        if t == 0:
                            pe.wait_ge(xT_ready, n * TPB + TPB)
                        for k in range(KD):
                            last = product(ps[:, 7, t * E:(t + 1) * E], pair(xT, al, k, tok), pair(chs, al, k, al),
                                           k == 0, k == KD - 1)
                        if t == TPB - 1:
                            last.then_inc(lg_done, 1)
                        if t >= 1:
                            kv(t - 1)

                    def q_rows(m):
                        if m < 2:
                            pe.wait_ge((k_read, v_read)[m], (n + 1) * TPB)
                        else:
                            pe.wait_ge(q_read[m % 2], n * 2 + 1)
                        for k in range(KD):
                            last = product(ps[:, 4 + m % 2, :], pair(wq, al, k, slice(m * P, (m + 1) * P)),
                                           pair(xT, al, k, al), k == 0, k == KD - 1)
                        last.then_inc(mm_done, 1)

                    for m in range(3):
                        q_rows(m)
                    turn_x(0, (n + 1) * TPB + 1)
                    pe.wait_ge(lg_read, n + 1)
                    turn_x(1, (n + 1) * TPB + 2)
                    q_rows(3)
                    kv(3)

                def exchange(k):
                    pe.wait_ge(route_dve, b * ROUTE + k + 1)

                def step(t, par):
                    if not isinstance(t, int) or t < NT:
                        pe.wait_ge(q_ready, b * NT + t + 1)
                        pe.wait_ge(o_raw, b * NT + t)
                        qh, ql = q_part(vv_hi, par), q_part(vv_lo, par)
                        for g in range(G):
                            last = product(ps[:, g, 0:264].rearrange("p (a c) -> p a c", a=2), (qh[:, g, :], ql[:, g, :]),
                                           (sum_hi[:, g, :, :], sum_lo[:, g, :, :]), True, True)
                        last.then_inc(ctx_done, 1)
                    if first(t, 1) and not (isinstance(t, int) and t > NT):
                        pe.wait_ge(o_ready, b * NT + t)
                        if first(t, 2):
                            pe.wait_ge(oT_ready, b * NT + t - 1)
                        for g in range(G):
                            last = nc.tensor.transpose(ps[:, 6, g * P:(g + 1) * P], work[:, 1, g, 0:P], ident)
                        last.then_inc(otr_done, 1)
                    if isinstance(t, int) and t == 0:
                        exchange(0)
                        for h in range(2):
                            last = nc.tensor.transpose(
                                ps[:, 7, h * P:(h + 1) * P],
                                probE[:, 4 * h:4 * h + 4, :].rearrange("p e t -> p (e t)"), ident)
                        last.then_inc(route_pe, 1)
                    if first(t, 2):
                        pe.wait_ge(oT_ready, b * NT + t - 1)
                        pe.wait_ge(fin, b * NT + t - 2)
                        for k in range(KD):
                            last = product(ps[:, 4 + par, :], pair((k_hi, k_lo), al, par, slice(k * P, (k + 1) * P)),
                                           pair(wo, al, k, al), k == 0, k == KD - 1)
                        last.then_inc(out_done, 1)
                    if first(t, 1) and not (isinstance(t, int) and t > BITS):
                        exchange(t)
                        nc.tensor.matmul(ps[:, 7, 0:2], same_block, cnt[:, 0:2], start=True, stop=True
                                         ).then_inc(route_pe, 1)

                pe.wait_ge(sums_ready, b + 1)
                for s in range(2):
                    pe.wait_ge(q_read[s], (b + 1) * (2 * NBLK))
                stage2_steps(pe, step)
                exchange(BITS + 1)
                nc.tensor.matmul(ps[:, 7, 0:4], same_block, cnt[:, 0:4], start=True, stop=True)
                nc.tensor.matmul(ps[:, 7, 4:6], earlier, cnt[:, 2:4], start=True, stop=True).then_inc(route_pe, 1)
                exchange(BITS + 2)
                nc.tensor.matmul(ps[:, 7, 0:2], earlier, cnt[:, 0:2], start=True, stop=True).then_inc(route_pe, 1)
                exchange(BITS + 3)
                for h in range(2):
                    last = nc.tensor.transpose(ps[:, 7, h * P:(h + 1) * P], mark[:, h, :], ident)
                last.then_inc(route_pe, 1)
                pe.wait_ge(fin, (b + 1) * NT)
                pe.wait_ge(rank_out, b + 1)

            def make_list(turn, c):
                if c == 0:
                    pe.wait_ge(idx_ready, turn)
                pe.wait_ge(list_dve, turn * 4 + (c + 1))
                for j in range(8):
                    last = nc.tensor.matmul(ps[:, 4, 0:16], one_lo[:, c % 2, j, :], pay[:, c * 8 + j, :],
                                            start=(c == 0 and j == 0), stop=(c == 3 and j == 7),
                                            skip_group_check=True)
                last.then_inc(list_pe, 1)

            def turn_rows(buf, loaded, before, tt):
                pe.wait_ge(rows_in[buf], loaded)
                if before is not None:
                    pe.wait_ge(xi_ready, before)
                for k in range(KD):
                    last = nc.tensor.transpose(ps[:, 6 + tt % 2, k * P:(k + 1) * P],
                                               rows[:, buf, tt, k * P:(k + 1) * P], ident)
                last.then_inc(gtr_done, 1)

            for b in range(B):
                for c in range(4):
                    make_list(b, c)
            for tt in range(TPB):
                turn_rows(0, 64, tt - 1 if tt >= 2 else None, tt)
            xi, w1s, w2s, hs = (xi_hi, xi_lo), (w1_hi, w1_lo), (w2_hi, w2_lo), (h_hi, h_lo)
            with pe.Fori(0, E) as e:
                for u in range(UNITS):
                    n = e * UNITS + u
                    pe.wait_ge(xi_ready, (n + 1) * TPB)
                    for m in range(KF):
                        if u == 0:
                            pe.wait_ge(w1_ready, e * KF + (m + 1))
                        pe.wait_ge(silu_done, n * KF + max(m - 1, 0))
                        for k in range(KD):
                            last = product(ps[:, m % 2, :], pair(w1s, al, k, slice(m * P, (m + 1) * P)),
                                           pair(xi, al, k, al), k == 0, k == KD - 1)
                        last.then_inc(up_done, 1)
                    for tt in range(TPB):
                        pe.wait_ge(y_ready, n * TPB + max(tt - 1, 0))
                        for k in range(KF):
                            if tt == 0:
                                pe.wait_ge(h_ready, n * KF + (k + 1))
                                if u == 0:
                                    pe.wait_ge(w2_ready, e * KF + (k + 1))
                            last = product(ps[:, 2 + tt % 2, :], pair(hs, al, k, slice(tt * P, (tt + 1) * P)),
                                           pair(w2s, al, k, al), k == 0, k == KF - 1)
                        last.then_inc(down_done, 1)
                        turn_rows((u + 1) % 2, e * 128 + ((u + 1) // 2 + 1) * 64, (n + 1) * TPB + (tt - 1), tt)
                        if u < B:
                            make_list(e * B + (B + u), tt)


_INS = ['L0_attn_x', 'L0_attn_W_qkv', 'L0_attn_b_qkv', 'L0_attn_W_out', 'L0_attn_b_out', 'L0_ffn_choice_w',
        'L0_ffn_w1', 'L0_ffn_w2']


def kernel(**inputs):
    import concourse.bacc as bacc
    from concourse.bass_utils import run_bass_kernel_spmd as run

    nc = bacc.Bacc("TRN2", target_bir_lowering=False, num_devices=1)
    arrays, args = {}, []
    table, bits = constants()
    for name, a in [(n, np.ascontiguousarray(inputs[n])) for n in _INS] + [("consts", table), ("bits", bits)]:
        arrays[f"in_{name}_dram"] = a
        args.append(nc.dram_tensor(f"in_{name}_dram", a.shape, mybir.dt.from_np(a.dtype), kind="ExternalInput").ap())
    args.append(nc.dram_tensor("out_0_dram", (B, L, D), F32, kind="ExternalOutput").ap())
    args.append(nc.dram_tensor("normed_rows", (B * L, ROW), F32, kind="Internal").ap())
    build(nc, *args)
    r = run(nc, [arrays], core_ids=[0])
    return r.results[0]["out_0_dram"]
```

```python
from contextlib import ExitStack

import numpy as np

import concourse.bass as bass
from concourse import mybir

ALU = mybir.AluOpType
ACT = mybir.ActivationFunctionType
AX = mybir.AxisListType
F32 = mybir.dt.float32
F32R = mybir.dt.float32r
BF16 = mybir.dt.bfloat16
I32 = mybir.dt.int32

P = 128
B, L, D = 2, 4096, 512
H, HD = 16, 32
E, F = 8, 1024
CAP = L * 2 // E
KD = D // P
G = KD
HPG = P // HD
KF = F // P
BLK = 512
TPB = BLK // P
NBLK = L // BLK
NT = L // P
ROW = D + E
LN_EPS = 1e-5
NORM_EPS = 1e-4
UNITS = B * CAP // BLK
HALVES = CAP // BLK
SLOT_TILES = CAP // P
BITS = 30
VW = P + 2
CON_LOADS = 4 + KD
HALF = D // 2
Q, K, V, O = range(4)
AHEAD, DMA_AHEAD = 1, 16
ROUTE = BITS + 4

C_IDENT, C_BLOCK, C_LOWER, C_IOTA, C_COS, C_SIN, C_EIGHT, C_TILE, C_PCOL, C_HEAD, C_END = np.cumsum(
    [0, P, P, P, P, NT, NT, 8, NT, 1, HPG]).tolist()


def constants():
    p = np.arange(P)
    c = np.zeros((P, C_END), np.float32)
    same = p[:, None] // NT == p[None, :] // NT
    c[:, C_IDENT:C_BLOCK] = np.eye(P)
    c[:, C_BLOCK:C_LOWER] = same
    c[:, C_LOWER:C_IOTA] = same & (p[:, None] < p[None, :])
    c[:, C_IOTA:C_COS] = p[None, :]
    angle = (np.float32(np.pi / 2) * np.arange(L, dtype=np.float32) / np.float32(L)).reshape(NT, P).T
    c[:, C_COS:C_SIN] = np.cos(angle)
    c[:, C_SIN:C_EIGHT] = np.sin(angle)
    c[:, C_EIGHT:C_TILE] = np.arange(8)
    c[:, C_TILE:C_PCOL] = np.arange(NT)
    c[:, C_PCOL] = p
    c[:, C_HEAD:C_END] = p[:, None] // HD == np.arange(HPG)[None, :]
    bits = np.zeros((P, NT), np.int32)
    bits[:, :BITS] = 1 << np.arange(BITS - 1, -1, -1)
    return c, bits


class Steps:

    def __init__(self, eng, sem):
        self.eng, self.sem, self.base, self.n, self.outer = eng, sem, 0, 0, []

    def did(self, ins):
        ins.then_inc(self.sem, 1)
        self.n += 1

    def wait(self):
        self.eng.wait_ge(self.sem, self.base + self.n)

    def enter(self, turn, per_turn):
        self.outer.append((self.base, self.n, per_turn))
        self.base, self.n = self.base + self.n + turn * per_turn, 0

    def leave(self, turns):
        base, n, per_turn = self.outer.pop()
        assert self.n == per_turn, f"{self.n} steps in a body of {per_turn}"
        self.base, self.n = base, n + turns * per_turn


def build(nc, x, w_qkv, b_qkv, w_out, b_out, choice_w, w1, w2, consts, bits, out, scratch):
    xf = x.rearrange("b l d -> (b l) d")
    of = out.rearrange("b l d -> (b l) d")
    with ExitStack() as ctx:
        def sem(name):
            return ctx.enter_context(nc.semaphore(name))

        def keep(name, shape, dt=F32):
            return ctx.enter_context(nc.sbuf_tensor(name, shape, dt))

        ps = ctx.enter_context(nc.psum_tensor("ps", [P, 8, 512], F32))

        con = keep("con", [P, C_END])
        bit = keep("bit", [P, NT], I32)
        rank_lo = keep("rank_lo", [P, B, E + 1, NT], BF16)
        rank_hi = keep("rank_hi", [P, B, E + 1, NT], BF16)
        iota_bf = keep("iota_bf", [P, P], BF16)
        zero = keep("zero", [P, 2 * VW], BF16)
        ident = con[:, C_IDENT:C_BLOCK]
        same_block = con[:, C_BLOCK:C_LOWER]
        earlier = con[:, C_LOWER:C_IOTA]

        with ExitStack() as early:
            def sb(name, shape, dt=F32):
                return early.enter_context(nc.sbuf_tensor(name, shape, dt))

            wq_hi = sb("wq_hi", [P, KD, 3 * D + E], F32R)
            wq_lo = sb("wq_lo", [P, KD, 3 * D + E], F32R)
            qT = sb("qT", [P, G, L])
            wo_hi = sb("wo_hi", [P, KD, D], F32R)
            wo_lo = sb("wo_lo", [P, KD, D], F32R)
            xT_hi = sb("xT_hi", [P, KD, BLK], F32R)
            xT_lo = sb("xT_lo", [P, KD, BLK], F32R)
            xq = sb("xq", [P, 2, D])
            xn = sb("xn", [P, TPB, D])
            k_hi = sb("k_hi", [P, 2, D], F32R)
            k_lo = sb("k_lo", [P, 2, D], F32R)
            vv_hi = sb("vv_hi", [P, 2, G, 2, 132], F32R)
            vv_lo = sb("vv_lo", [P, 2, G, 2, 132], F32R)
            work = sb("work", [P, 2, G, 132])
            xo = sb("xo", [P, 2, D])
            bk = sb("bk", [P, D])
            bv = sb("bv", [P, D])
            bo = sb("bo", [P, D])
            bq = sb("bq", [P, KD])
            ch = sb("ch", [P, KD, E])
            logit = sb("logit", [P, NT, E])
            prob = sb("prob", [P, NT, E])
            probE = sb("probE", [P, E, NT])
            probT = sb("probT", [P, 2, P])
            mark = sb("mark", [P, 2, P])
            stats = sb("stats", [P, 2, 6])
            mv = sb("mv", [P, 2, 2])
            var1 = sb("var1", [P, 2])
            std = sb("std", [P, 2])
            rstd = sb("rstd", [P, 2])
            newt = sb("newt", [P, 2])
            rden = sb("rden", [P, G, HPG])
            top = sb("top", [P, NT])
            thr = sb("thr", [P, 2], I32)
            cand = sb("cand", [P, 2], I32)
            hit = sb("hit", [P, 2], I32)
            cnt = sb("cnt", [P, 4])
            pre = sb("pre", [P, 4])
        kf = work[:, 0, :, :].rearrange("p g c -> p (g c)")[:, 0:D]
        vf = work[:, 1, :, :]
        sum_hi, sum_lo = vv_hi[:, 0, :, :, :], vv_lo[:, 0, :, :, :]

        def raw_weights(part):
            return qT[:, part, L // 2:].rearrange("p (k d) -> p k d", k=KD)

        def q_part(pair, par):
            return pair[:, 1, :, :, :].rearrange("p g t c -> p (g t c)")[:, par * D:(par + 1) * D].rearrange(
                "p (g c) -> p g c", g=G)

        with ExitStack() as late:
            def sb(name, shape, dt=F32):
                return late.enter_context(nc.sbuf_tensor(name, shape, dt))

            w1_raw = sb("w1_raw", [P, KD, F])
            w2_raw = sb("w2_raw", [P, KF, D])
            w1_hi = sb("w1_hi", [P, KD, F], F32R)
            w1_lo = sb("w1_lo", [P, KD, F], F32R)
            w2_hi = sb("w2_hi", [P, KF, D], F32R)
            w2_lo = sb("w2_lo", [P, KF, D], F32R)
            rows = sb("rows", [P, 2, TPB, ROW])
            xi_hi = sb("xi_hi", [P, KD, BLK], F32R)
            xi_lo = sb("xi_lo", [P, KD, BLK], F32R)
            h_hi = sb("h_hi", [P, KF, BLK], F32R)
            h_lo = sb("h_lo", [P, KF, BLK], F32R)
            hf = sb("hf", [P, 2, BLK])
            y = sb("y", [P, TPB, D])
            one_lo = sb("one_lo", [P, 2, 8, P], BF16)
            one_hi = sb("one_hi", [P, NT, 8], BF16)
            pay = sb("pay", [P, NT, 16], BF16)
            idx_f = sb("idx_f", [P, 8])
            idx_next = sb("idx_next", [P, B * SLOT_TILES], I32)
            idx = sb("idx", [P, B * SLOT_TILES], I32)

        table_in, con_in = sem("table_in"), sem("con_in")
        w_in = [sem(f"w{part}_in") for part in "qkvo"]
        x_in, xn_ready = sem("x_in"), sem("xn_ready")
        xn_stored = [sem(f"xn_stored{s}") for s in range(2)]
        dve_steps = sem("dve_steps")
        wo_ready = sem("wo_ready")
        w_ready, w_hi_ready = sem("w_ready"), sem("w_hi_ready")
        var_ready, std_ready = sem("var_ready"), sem("std_ready")
        tr_done, xT_hi_ready, xT_ready = sem("tr_done"), sem("xT_hi_ready"), sem("xT_ready")
        mm_done, lg_read = sem("mm_done"), sem("lg_read")
        k_read, v_read = sem("k_read"), sem("v_read")
        q_read = sem("q_read")
        k_hi_ready, k_ready, vv_ready = sem("k_hi_ready"), sem("k_ready"), sem("vv_ready")
        kv_zero, kv_done = sem("kv_zero"), sem("kv_done")
        sums_ready = sem("sums_ready")
        q_hi_ready, q_ready, ctx_done = sem("q_hi_ready"), sem("q_ready"), sem("ctx_done")
        sin_ready, o_raw, o_ready = sem("sin_ready"), sem("o_raw"), sem("o_ready")
        otr_done, oT_hi_ready, oT_ready = sem("otr_done"), sem("oT_hi_ready"), sem("oT_ready")
        out_done, res_ready, fin = sem("out_done"), sem("res_ready"), sem("fin")
        xo_in = [sem(f"xo_in{s}") for s in range(2)]
        out_stored = [sem(f"out_stored{s}") for s in range(2)]
        soft_sub, soft_exp, prob_ready, prob_stored = sem("soft_sub"), sem("soft_exp"), sem("prob_ready"), sem("prob_stored")
        route_dve, route_pe = sem("route_dve"), sem("route_pe")
        rank_out = sem("rank_out")
        w1_in, w2_in = sem("w1_in"), sem("w2_in")
        w1_hi_ready, w1_ready, w2_hi_ready, w2_ready = sem("w1_hi_ready"), sem("w1_ready"), sem("w2_hi_ready"), sem("w2_ready")
        rows_in = [sem(f"rows_in{s}") for s in range(2)]
        list_dve, list_pe, idx_ready, idx_copied = sem("list_dve"), sem("list_pe"), sem("idx_ready"), sem("idx_copied")
        gtr_done, xi_hi_ready, xi_ready = sem("gtr_done"), sem("xi_hi_ready"), sem("xi_ready")
        up_done, silu_done, h_ready = sem("up_done"), sem("silu_done"), sem("h_ready")
        down_done, y_ready = sem("down_done"), sem("y_ready")
        added = [sem(f"added{b}") for b in range(B)]

        block = ctx.enter_context(nc.Block())

        def first(t, n):
            return not isinstance(t, int) or t >= n

        def apart(eng):
            eng.nop(nofuse=True)

        def stage2_steps(eng, step):
            for t in range(2):
                step(t, t % 2)
            with eng.Fori(0, (NT - 4) // 2) as j:
                for s in range(2):
                    step(j * 2 + (2 + s), s)
            for t in range(NT - 2, NT + 2):
                step(t, t % 2)

        @block.sync
        def _(sp):
            for signal in (mm_done, kv_done, vv_ready, q_read, k_read, v_read, lg_read, o_raw, otr_done, out_done, fin, list_pe, idx_ready,
                           silu_done, h_ready, down_done, y_ready):
                sp.sem_inc(signal, AHEAD)
            for signal in (prob_stored, *out_stored):
                sp.sem_inc(signal, DMA_AHEAD)
            def store_normed(j, s):
                sp.wait_ge(xn_ready, j * TPB + (2 * s + 2))
                sp.dma_start(scratch[bass.ds(j * BLK + 2 * s * P, 2 * P), 0:D].rearrange("(t p) d -> p t d", p=P),
                             xn[:, 2 * s:2 * s + 2, :]).then_inc(xn_stored[s], 16)

            def load_x(row):
                sp.dma_start(xq[:, :, :], xf[bass.ds(row, 2 * P), :].rearrange("(t p) d -> p t d", p=P)
                             ).then_inc(x_in, 16)

            def load_weights(part):
                src = w_out if part == O else w_qkv[:, part * D:(part + 1) * D]
                sp.dma_start(raw_weights(part), src.rearrange("(k p) d -> p k d", p=P)).then_inc(w_in[part], 16)

            load_x(0)
            sp.dma_start(xo[:, :, :], xf[2 * P:4 * P, :].rearrange("(t p) d -> p t d", p=P)).then_inc(x_in, 16)
            sp.dma_start(con[:, :], consts).then_inc(table_in, 16)
            sp.dma_start(bit[:, :], bits).then_inc(table_in, 16)
            load_weights(Q)
            load_weights(V)
            with nc.allow_non_contiguous_dma("small transposed loads"):
                sp.dma_start(bq[:, :], b_qkv[0:D].rearrange("(m p) -> p m", p=P)).then_inc(con_in, 16)
                for k in range(KD):
                    sp.dma_start(ch[:, k, :], choice_w[:, k * P:(k + 1) * P].rearrange("e p -> p e")
                                 ).then_inc(con_in, 16)
            for n, dst in ((1, bk), (2, bv)):
                sp.dma_start(dst[:, :], b_qkv[n * D:(n + 1) * D].rearrange("(a d) -> a d", a=1).to_broadcast([P, D])
                             ).then_inc(con_in, 16)
            sp.dma_start(bo[:, :], b_out.rearrange("(a d) -> a d", a=1).to_broadcast([P, D])).then_inc(con_in, 16)
            load_weights(K)
            load_weights(O)
            store_normed(0, 0)
            store_normed(0, 1)
            def load_w1(e):
                sp.dma_start(w1_raw[:, :, :], w1[bass.ds(e, 1), :, :].rearrange("e (k p) f -> p (e k) f", p=P)
                             ).then_inc(w1_in, 16)

            def load_w2(e):
                sp.dma_start(w2_raw[:, :, :], w2[bass.ds(e, 1), :, :].rearrange("e (k p) d -> p (e k) d", p=P)
                             ).then_inc(w2_in, 16)

            for b in range(B):
                with sp.Fori(0, NBLK) as i:
                    nxt = b * NBLK + i + 1
                    src = (nxt % (B * NBLK)) * BLK
                    for s in range(2):
                        sp.wait_ge(xn_ready, nxt * TPB + 2 * s)
                        load_x(src + 2 * s * P)
                        sp.wait_ge(xn_ready, nxt * TPB + (2 * s + 2))
                        sp.dma_start(scratch[bass.ds(src + 2 * s * P, 2 * P), 0:D].rearrange("(t p) d -> p t d", p=P),
                                     xn[:, 2 * s:2 * s + 2, :]).then_inc(xn_stored[s], 16)

                if b == B - 1:
                    sp.wait_ge(kv_done, AHEAD + B * NT)
                    load_w1(0)
                    load_w2(0)

                def load_res(t, par):
                    sp.dma_start(xo[:, par, :], xf[bass.ds(b * L + t * P, P), :]).then_inc(xo_in[par], 16)

                for t in range(2):
                    sp.wait_ge(out_stored[t], DMA_AHEAD + b * (NT // 2) * 16)
                    load_res(t, t)
                sp.wait_ge(prob_ready, b + 1)
                sp.dma_start(scratch[bass.ds(b * L, L), D:ROW].rearrange("(t p) e -> p t e", p=P),
                             prob[:, :, :]).then_inc(prob_stored, 16)

                def store_out(t, par):
                    sp.wait_ge(fin, AHEAD + b * NT + t + 1)
                    sp.dma_start(of[bass.ds(b * L + t * P, P), :], xo[:, par, :]).then_inc(out_stored[par], 16)

                with sp.Fori(0, NT // 2 - 1) as j:
                    for par in range(2):
                        store_out(j * 2 + par, par)
                        sp.wait_ge(out_stored[par], DMA_AHEAD + (b * (NT // 2) + j + 1) * 16)
                        load_res(j * 2 + (2 + par), par)
                for par in range(2):
                    store_out(NT - 2 + par, par)

            with sp.Fori(0, E) as e:
                nxt_e = (e + 1) % E
                sp.wait_ge(w1_ready, (e + 1) * KF)
                load_w1(nxt_e)
                sp.wait_ge(w2_ready, (e + 1) * KF)
                load_w2(nxt_e)
            sp.wait_ge(w1_in, 16 * (E + 1))
            sp.wait_ge(w2_in, 16 * (E + 1))
            for s in range(2):
                sp.wait_ge(xn_stored[s], 16 * (B * NBLK + 1))
                sp.wait_ge(out_stored[s], DMA_AHEAD + 16 * B * NT // 2)
            sp.wait_ge(prob_stored, DMA_AHEAD + 16 * B)
            for b in range(B):
                sp.wait_ge(added[b], 16 * E * SLOT_TILES)

        @block.gpsimd
        def _(pool):
            pool.wait_ge(w_hi_ready, 4)
            nc.gpsimd.tensor_tensor(wo_lo[:, :, :], raw_weights(O), wo_hi[:, :, :].bitcast(F32), ALU.subtract
                                    ).then_inc(wo_ready, 1)
            pool.wait_ge(con_in, CON_LOADS * 16)
            with pool.Fori(0, B) as b:
                with pool.Fori(0, NT // 2) as j:
                    for par in range(2):
                        n = b * NT + j * 2 + par
                        pool.wait_ge(xo_in[par], (b * (NT // 2) + j + 1) * 16)
                        nc.gpsimd.tensor_tensor(xo[:, par, :], xo[:, par, :], bo[:, :], ALU.add).then_inc(res_ready, 1)

            def gather(table, col, buf, tt):
                nc.gpsimd.indirect_dma_start(rows[:, buf, tt, :], None, scratch[:, :],
                                             bass.IndirectOffsetOnAxis(ap=table[:, col:col + 1], axis=0)
                                             ).then_inc(rows_in[buf], 16)

            def copy_list():
                nc.gpsimd.tensor_copy(idx[:, :], idx_next[:, :]).then_inc(idx_copied, 1)

            for s in range(2):
                pool.wait_ge(xn_stored[s], 16 * (B * NBLK + 1))
                pool.wait_ge(out_stored[s], DMA_AHEAD + 16 * B * NT // 2)
            pool.wait_ge(prob_stored, DMA_AHEAD + 16 * B)
            pool.wait_ge(idx_ready, AHEAD + 1)
            for tt in range(TPB):
                gather(idx_next, tt, 0, tt)
            pool.wait_ge(idx_ready, AHEAD + B)
            copy_list()
            with pool.Fori(0, E) as e:
                for u in range(UNITS):
                    b = u // HALVES
                    pool.wait_ge(y_ready, AHEAD + e * (UNITS * TPB) + u * TPB)
                    if u == UNITS - 1:
                        pool.wait_ge(idx_ready, AHEAD + e * B + 2 * B)
                    elif u == 0:
                        pool.wait_ge(idx_copied, e + 1)
                    apart(pool)
                    for tt in range(TPB):
                        if u == UNITS - 1:
                            gather(idx_next, tt, 0, tt)
                        else:
                            gather(idx, (u + 1) * TPB + tt, (u + 1) % 2, tt)
                    for tt in range(TPB):
                        pool.wait_ge(y_ready, AHEAD + e * (UNITS * TPB) + (u * TPB + tt + 1))
                        apart(pool)
                        nc.gpsimd.indirect_dma_start(
                            of[:, :], bass.IndirectOffsetOnAxis(ap=idx[:, u * TPB + tt:u * TPB + tt + 1], axis=0),
                            y[:, tt, :], None, compute_op=ALU.add).then_inc(added[b], 16)
                for b in range(B):
                    pool.wait_ge(added[b], (e + 1) * (16 * SLOT_TILES))
                pool.wait_ge(rows_in[0], e * (64 * UNITS // 2) + 64 * (UNITS // 2 + 1))
                apart(pool)
                copy_list()
            pool.wait_ge(rows_in[0], 64 * (E * UNITS // 2 + 1))

        @block.scalar
        def _(act):
            def sqrt(j, s):
                act.wait_ge(var_ready, j * 2 + s + 1)
                nc.scalar.activation(std[:, :], var1[:, :], ACT.Sqrt).then_inc(std_ready, 1)

            def turned_hi(j, t, matmuls, bank=7):
                act.wait_ge(tr_done, j * TPB + t + 1)
                if matmuls is not None:
                    act.wait_ge(mm_done, AHEAD + matmuls)
                nc.scalar.copy(xT_hi[:, :, t * P:(t + 1) * P],
                               ps[:, bank, :].rearrange("p (k c) -> p k c", k=KD)).then_inc(xT_hi_ready, 1)

            sqrt(0, 0)
            sqrt(0, 1)
            for part in (Q, V, K):
                act.wait_ge(w_in[part], 16)
                if part == V:
                    act.wait_ge(con_in, CON_LOADS * 16)
                    nc.scalar.copy(wq_hi[:, :, 3 * D:3 * D + E], ch[:, :, :])
                nc.scalar.copy(wq_hi[:, :, part * D:(part + 1) * D], raw_weights(part)).then_inc(w_hi_ready, 1)
                if part == Q:
                    for t in range(TPB):
                        turned_hi(0, t, None, 4 + t)
            act.wait_ge(w_in[O], 16)
            nc.scalar.copy(wo_hi[:, :, :], raw_weights(O)).then_inc(w_hi_ready, 1)
            with act.Fori(0, B) as b:
                with act.Fori(0, NBLK) as i:
                    n = b * NBLK + i

                    def q_out(m):
                        act.wait_ge(mm_done, AHEAD + n * 12 + (m + 1))
                        nc.scalar.activation(qT[:, m, bass.ds(i * BLK, BLK)], ps[:, (5, 6, 5, 4)[m], :], ACT.Relu,
                                             bias=bq[:, m:m + 1]).then_inc(q_read, 1)

                    sqrt(n + 1, 0)
                    q_out(0)
                    q_out(1)
                    q_out(2)
                    sqrt(n + 1, 1)
                    q_out(3)
                    for t in range(TPB):
                        turned_hi(n + 1, t, n * 12 + (2 * t + 6))
                        act.wait_ge(k_read, AHEAD + n * TPB + t + 1)
                        act.wait_ge(kv_done, AHEAD + n * TPB + max(t - 1, 0))
                        nc.scalar.activation(k_hi[:, t % 2, :], kf, ACT.Relu).then_inc(k_hi_ready, 1)

                def q_hi(t, par):
                    if first(t, 2):
                        act.wait_ge(ctx_done, b * NT + t - 1)
                    nc.scalar.copy(q_part(vv_hi, par), qT[:, :, bass.ds(t * P, P)]).then_inc(q_hi_ready, 1)

                act.wait_ge(soft_sub, b + 1)
                nc.scalar.activation(logit[:, :, :], logit[:, :, :], ACT.Exp).then_inc(soft_exp, 1)
                act.wait_ge(kv_done, AHEAD + (b + 1) * NT)
                q_hi(0, 0)

                def step(t, par):
                    if not isinstance(t, int) or t < NT - 1:
                        q_hi(t + 1, 1 - par)
                    if not isinstance(t, int) or t < NT:
                        act.wait_ge(ctx_done, b * NT + t + 1)
                        act.wait_ge(o_raw, AHEAD + b * NT + t)
                        nc.scalar.activation(work[:, 0, :, :], ps[:, 0:4, 132:264], ACT.Copy,
                                             scale=con[:, bass.ds(C_SIN + t, 1)]).then_inc(sin_ready, 1)
                    if first(t, 1) and not (isinstance(t, int) and t > NT):
                        act.wait_ge(otr_done, AHEAD + b * NT + t)
                        if first(t, 3):
                            act.wait_ge(out_done, AHEAD + b * NT + t - 2)
                        nc.scalar.copy(k_hi[:, 1 - par, :], ps[:, 6, :]).then_inc(oT_hi_ready, 1)

                stage2_steps(act, step)

            def w1_high(e, m):
                sl = slice(m * P, (m + 1) * P)
                nc.scalar.copy(w1_hi[:, :, sl], w1_raw[:, :, sl]).then_inc(w1_hi_ready, 1)

            def rows_hi(unit, tt):
                act.wait_ge(gtr_done, unit * TPB + tt + 1)
                nc.scalar.copy(xi_hi[:, :, tt * P:(tt + 1) * P],
                               ps[:, 6 + tt % 2, :].rearrange("p (k c) -> p k c", k=KD)).then_inc(xi_hi_ready, 1)

            act.wait_ge(w1_in, 16)
            for m in range(KF):
                w1_high(0, m)
            for tt in range(TPB):
                rows_hi(0, tt)
            with act.Fori(0, E) as e:
                for u in range(UNITS):
                    n = e * UNITS + u
                    for m in range(KF):
                        act.wait_ge(up_done, n * KF + m + 1)
                        act.wait_ge(h_ready, AHEAD + n * KF + max(m - 1, 0))
                        nc.scalar.activation(hf[:, m % 2, :], ps[:, m % 2, :], ACT.Silu).then_inc(silu_done, 1)
                        if u == 0:
                            if m == 0:
                                act.wait_ge(w2_in, (e + 1) * 16)
                                act.wait_ge(down_done, AHEAD + n * TPB)
                            nc.scalar.copy(w2_hi[:, m, :], w2_raw[:, m, :]).then_inc(w2_hi_ready, 1)
                    if u == 0:
                        act.wait_ge(idx_copied, e + 1)
                    else:
                        before = u - 1
                        act.wait_ge(added[before // HALVES],
                                    (e * SLOT_TILES + (before % HALVES + 1) * TPB) * 16)
                    for tt in range(TPB):
                        rows_hi(n + 1, tt)
                        act.wait_ge(down_done, AHEAD + n * TPB + tt + 1)
                        apart(act)
                        nc.scalar.activation(y[:, tt, :], ps[:, 2 + tt % 2, :], ACT.Copy,
                                             scale=rows[:, u % 2, tt, bass.ds(D + e, 1)]).then_inc(y_ready, 1)
                        if u == UNITS - 1:
                            if tt == 0:
                                act.wait_ge(w1_in, e * 16 + 32)
                            for m in (2 * tt, 2 * tt + 1):
                                w1_high(e, m)

        @block.vector
        def _(dve):
            me = Steps(dve, dve_steps)

            def norm_half(j, s, src, loads, reuse):
                dve.wait_ge(x_in, loads * 16)
                for tt in range(2):
                    me.did(nc.vector.bn_stats(stats[:, tt, :], src[:, tt, :]))
                me.wait()
                apart(dve)
                for tt in range(2):
                    me.did(nc.vector.bn_aggr(mv[:, tt, :], stats[:, tt, :]))
                me.wait()
                nc.vector.tensor_scalar(var1[:, :], mv[:, :, 1], LN_EPS, None, ALU.add).then_inc(var_ready, 1)
                dve.wait_ge(std_ready, j * 2 + s + 1)
                me.did(nc.vector.reciprocal(rstd[:, :], std[:, :]))
                me.wait()
                me.did(nc.vector.tensor_tensor(newt[:, :], rstd[:, :], rstd[:, :], ALU.mult))
                me.wait()
                me.did(nc.vector.tensor_tensor(newt[:, :], newt[:, :], var1[:, :], ALU.mult))
                me.wait()
                me.did(nc.vector.tensor_scalar(newt[:, :], newt[:, :], -0.5, 1.5, ALU.mult, ALU.add))
                me.wait()
                me.did(nc.vector.tensor_tensor(rstd[:, :], rstd[:, :], newt[:, :], ALU.mult))
                me.wait()
                if reuse:
                    dve.wait_ge(xn_stored[s], j * 16)
                    dve.wait_ge(tr_done, j * TPB - 2 + 2 * s)
                for tt in range(2):
                    nc.vector.tensor_scalar(xn[:, 2 * s + tt, :], src[:, tt, :], mv[:, tt, 0:1], rstd[:, tt:tt + 1],
                                            ALU.subtract, ALU.mult).then_inc(xn_ready, 1)

            def turned_lo(j, t, bank=7):
                dve.wait_ge(xT_hi_ready, j * TPB + t + 1)
                sl = slice(t * P, (t + 1) * P)
                nc.vector.tensor_tensor(xT_lo[:, :, sl], ps[:, bank, :].rearrange("p (k c) -> p k c", k=KD),
                                        xT_hi[:, :, sl].bitcast(F32), ALU.subtract).then_inc(xT_ready, 1)

            norm_half(0, 0, xq, 2, False)
            norm_half(0, 1, xo, 2, False)
            dve.wait_ge(table_in, 2 * 16)
            nc.vector.tensor_copy(iota_bf[:, :], con[:, C_IOTA:C_COS])
            nc.vector.memset(zero[:, :], 0.0)
            for step, part in enumerate((Q, V, K)):
                dve.wait_ge(w_hi_ready, step + 1)
                if part == V:
                    nc.vector.tensor_tensor(wq_lo[:, :, 3 * D:3 * D + E], ch[:, :, :],
                                            wq_hi[:, :, 3 * D:3 * D + E].bitcast(F32), ALU.subtract)
                if part == K:
                    nc.vector.memset(rank_lo[:, :, E:E + 1, :], -1.0)
                    nc.vector.memset(rank_hi[:, :, E:E + 1, :], -1.0)
                hi, lo = (a[:, :, part * D:(part + 1) * D] for a in (wq_hi, wq_lo))
                nc.vector.tensor_tensor(lo[:, :, :], raw_weights(part), hi[:, :, :].bitcast(F32), ALU.subtract
                                        ).then_inc(w_ready, 1)
                if part == Q:
                    for t in range(TPB):
                        turned_lo(0, t, 4 + t)

            N_BLOCK, N_PAIR, N_BATCH, N_EXPERT = 2 * 9 + 2 * TPB, 10, 389, 40

            with dve.Fori(0, B) as b:
                me.enter(b, N_BATCH)
                me.did(nc.vector.memset(vf[:, :, P:P + 1], 1.0))
                me.did(nc.vector.memset(vf[:, :, P + 1:VW], 0.0))
                me.wait()
                apart(dve)
                with dve.Fori(0, NBLK) as i:
                    me.enter(i, N_BLOCK)
                    n = b * NBLK + i
                    for s in range(2):
                        norm_half(n + 1, s, xq, n * 2 + (s + 3), True)
                    for t in range(TPB):
                        par = t % 2
                        dve.wait_ge(mm_done, AHEAD + n * 12 + (2 * t + 5))
                        nc.vector.tensor_tensor(vf[:, :, 0:P].rearrange("p (a g) c -> p a g c", a=2),
                                                ps[:, 5:7, 0:HALF].rearrange("p a (g c) -> p a g c", c=P),
                                                bv[:, :].rearrange("p (a g c) -> p a g c", a=2, c=P),
                                                ALU.add).then_inc(v_read, 1)
                        nc.vector.tensor_copy(logit[:, bass.ds(i * TPB + t, 1), :].rearrange("p t e -> p (t e)"),
                                              ps[:, 6, HALF:HALF + E]).then_inc(lg_read, 1)
                        dve.wait_ge(v_read, AHEAD + n * TPB + t + 1)
                        v = vf[:, :, 0:VW]
                        for trig, c in ((0, C_COS), (1, C_SIN)):
                            me.did(nc.vector.tensor_scalar(vv_hi[:, par, :, trig, 0:VW], v,
                                                           con[:, bass.ds(c + i * TPB + t, 1)], None, ALU.mult))
                        me.wait()
                        for trig, c in ((0, C_COS), (1, C_SIN)):
                            last = nc.vector.scalar_tensor_tensor(
                                vv_lo[:, par, :, trig, 0:VW], v, con[:, bass.ds(c + i * TPB + t, 1)],
                                vv_hi[:, par, :, trig, 0:VW].bitcast(F32), ALU.mult, ALU.subtract)
                        last.then_inc(vv_ready, 1)
                        dve.wait_ge(mm_done, AHEAD + n * 12 + (2 * t + 6))
                        nc.vector.tensor_tensor(kf, ps[:, 4, :], bk[:, :], ALU.add).then_inc(k_read, 1)
                        turned_lo(n + 1, t)
                        dve.wait_ge(k_hi_ready, n * TPB + t + 1)
                        nc.vector.scalar_tensor_tensor(k_lo[:, par, :], kf, 0.0, k_hi[:, par, :].bitcast(F32),
                                                       ALU.max, ALU.subtract).then_inc(k_ready, 1)
                    me.leave(NBLK)

                def softmax_start():
                    me.did(nc.vector.tensor_reduce(top[:, :], logit[:, :, :], AX.X, ALU.max))
                    me.wait()
                    nc.vector.tensor_tensor(logit[:, :, :], logit[:, :, :],
                                            top[:, :].rearrange("p (t e) -> p t e", e=1).to_broadcast([P, NT, E]),
                                            ALU.subtract).then_inc(soft_sub, 1)

                def softmax_end():
                    dve.wait_ge(soft_exp, b + 1)
                    me.did(nc.vector.tensor_reduce(top[:, :], logit[:, :, :], AX.X, ALU.add))
                    me.wait()
                    me.did(nc.vector.reciprocal(top[:, :], top[:, :]))
                    me.wait()
                    dve.wait_ge(prob_stored, DMA_AHEAD + b * 16)
                    nc.vector.tensor_tensor(prob[:, :, :], logit[:, :, :],
                                            top[:, :].rearrange("p (t e) -> p t e", e=1).to_broadcast([P, NT, E]),
                                            ALU.mult).then_inc(prob_ready, 1)
                    dve.wait_ge(prob_ready, b + 1)
                    nc.vector.tensor_copy(probE[:, :, :].rearrange("p e t -> p t e"), prob[:, :, :]
                                          ).then_inc(route_dve, 1)

                softmax_start()
                dve.wait_ge(kv_done, AHEAD + (b + 1) * NT)
                sums = work[:, :, :, :].rearrange("p a g c -> p (a g c)").rearrange("p (g t c) -> p g t c", g=G, t=2)
                raw_sums = ps[:, 0:G, 0:2 * VW].rearrange("p g (t c) -> p g t c", t=2)
                me.did(nc.vector.tensor_tensor(
                    sums[:, :, :, 0:P], raw_sums[:, :, :, 0:P],
                    same_block.rearrange("p (a b c) -> p a b c", a=1, b=1).to_broadcast([P, G, 2, P]), ALU.mult))
                me.did(nc.vector.tensor_tensor(
                    sums[:, :, :, P:P + HPG], raw_sums[:, :, :, P:P + 1].to_broadcast([P, G, 2, HPG]),
                    con[:, C_HEAD:C_END].rearrange("p (a b c) -> p a b c", a=1, b=1).to_broadcast([P, G, 2, HPG]),
                    ALU.mult))
                me.wait()
                me.did(nc.vector.tensor_copy(sum_hi, sums))
                me.wait()
                nc.vector.tensor_tensor(sum_lo, sums, sum_hi.bitcast(F32), ALU.subtract).then_inc(sums_ready, 1)

                def q_lo(t, par):
                    dve.wait_ge(q_hi_ready, b * NT + t + 1)
                    nc.vector.tensor_tensor(q_part(vv_lo, par), qT[:, :, bass.ds(t * P, P)],
                                            q_part(vv_hi, par).bitcast(F32), ALU.subtract).then_inc(q_ready, 1)

                q_lo(0, 0)
                softmax_end()

                def search_start():
                    dve.wait_ge(route_pe, b * ROUTE + 1)
                    me.did(nc.vector.tensor_copy(probT[:, :, :].rearrange("p h c -> p (h c)"), ps[:, 7, 0:2 * P]))
                    me.did(nc.vector.memset(thr[:, :], 0))
                    me.wait()

                def count(s):
                    me.did(nc.vector.tensor_tensor(cand[:, :], thr[:, :], bit[:, bass.ds(s, 1)].to_broadcast([P, 2]),
                                                   ALU.bitwise_or))
                    me.wait()
                    for h in range(2):
                        last = nc.vector.tensor_scalar(mark[:, h, :], probT[:, h, :], cand[:, h:h + 1].bitcast(F32),
                                                       None, ALU.is_ge, ALU.add, accum_out=cnt[:, h:h + 1])
                    last.then_inc(route_dve, 1)

                def settle(s):
                    dve.wait_ge(route_pe, b * ROUTE + s + 2)
                    me.did(nc.vector.tensor_scalar(hit[:, :], ps[:, 7, 0:2], float(CAP) - 0.5, None, ALU.is_ge))
                    me.wait()
                    apart(dve)
                    me.did(nc.vector.copy_predicated(thr[:, :], hit[:, :], cand[:, :]))
                    me.wait()

                above, equal = logit[:, :, :].rearrange("p t e -> p (t e)"), probE[:, :, :].rearrange("p e t -> p (e t)")
                above, equal = (a.rearrange("p (h c) -> p h c", h=2) for a in (above, equal))

                def rank_marks():
                    for h in range(2):
                        t_h = thr[:, h:h + 1].bitcast(F32)
                        me.did(nc.vector.tensor_scalar(above[:, h, :], probT[:, h, :], t_h, None, ALU.is_gt, ALU.add,
                                                       accum_out=cnt[:, h:h + 1]))
                        last = nc.vector.tensor_scalar(equal[:, h, :], probT[:, h, :], t_h, None, ALU.is_equal, ALU.add,
                                                       accum_out=cnt[:, 2 + h:3 + h])
                    last.then_inc(route_dve, 1)

                def rank_chosen():
                    dve.wait_ge(route_pe, b * ROUTE + BITS + 2)
                    me.did(nc.vector.tensor_scalar(pre[:, 0:2], ps[:, 7, 0:2], -1.0, float(CAP), ALU.mult, ALU.add))
                    me.did(nc.vector.tensor_copy(pre[:, 2:4], ps[:, 7, 4:6]))
                    me.wait()
                    for h in range(2):
                        me.did(nc.vector.tensor_tensor_scan(mark[:, h, :], equal[:, h, :], equal[:, h, :],
                                                            pre[:, 2 + h:3 + h], ALU.add, ALU.max))
                    me.wait()
                    for h in range(2):
                        me.did(nc.vector.scalar_tensor_tensor(mark[:, h, :], mark[:, h, :], pre[:, h:h + 1],
                                                              equal[:, h, :], ALU.is_le, ALU.mult))
                    me.wait()
                    me.did(nc.vector.tensor_tensor(above, above, mark[:, :, :], ALU.add))
                    me.wait()
                    nc.vector.tensor_reduce(cnt[:, 0:2], above, AX.X, ALU.add).then_inc(route_dve, 1)

                def rank_number():
                    dve.wait_ge(route_pe, b * ROUTE + BITS + 3)
                    me.did(nc.vector.tensor_copy(pre[:, 2:4], ps[:, 7, 0:2]))
                    me.wait()
                    for h in range(2):
                        me.did(nc.vector.tensor_tensor_scan(mark[:, h, :], above[:, h, :], above[:, h, :],
                                                            pre[:, 2 + h:3 + h], ALU.add, ALU.max))
                    me.wait()
                    me.did(nc.vector.tensor_tensor(mark[:, :, :], mark[:, :, :], above, ALU.mult))
                    me.wait()
                    nc.vector.tensor_scalar(mark[:, :, :], mark[:, :, :], -1.0, None, ALU.add).then_inc(route_dve, 1)

                def rank_split():
                    dve.wait_ge(route_pe, b * ROUTE + BITS + 4)
                    rank_i = probT[:, :, :].rearrange("p h c -> p (h c)").bitcast(I32)
                    part_i = mark[:, :, :].rearrange("p h c -> p (h c)").bitcast(I32)
                    nc.vector.tensor_copy(rank_i, ps[:, 7, 0:2 * P]).then_inc(rank_out, 1)
                    dve.wait_ge(rank_out, b + 1)
                    for op, by, dst in ((ALU.bitwise_and, P - 1, rank_lo), (ALU.arith_shift_right, 7, rank_hi)):
                        me.did(nc.vector.tensor_scalar(part_i, rank_i, by, None, op))
                        me.wait()
                        me.did(nc.vector.tensor_copy(dst[:, bass.ds(b, 1), 0:E, :].rearrange("p b e t -> p (b e t)"),
                                                     part_i))
                        me.wait()

                def step(t, par):
                    if first(t, 2) and not (isinstance(t, int) and t >= NT):
                        settle(t - 2)
                        if not isinstance(t, int) or t < NT - 1:
                            count(t - 1)
                    if not isinstance(t, int) or t < NT - 1:
                        q_lo(t + 1, 1 - par)
                    if not isinstance(t, int) or t < NT:
                        o = work[:, 1, :, :]
                        dve.wait_ge(sin_ready, b * NT + t + 1)
                        dve.wait_ge(otr_done, AHEAD + b * NT + t)
                        nc.vector.scalar_tensor_tensor(
                            o, ps[:, 0:4, 0:132], con[:, bass.ds(C_COS + t, 1)], work[:, 0, :, :],
                            ALU.mult, ALU.add).then_inc(o_raw, 1)
                        dve.wait_ge(o_raw, AHEAD + b * NT + t + 1)
                        me.did(nc.vector.tensor_scalar(rden[:, :, :], o[:, :, P:P + HPG], NORM_EPS, None, ALU.add))
                        me.wait()
                        me.did(nc.vector.reciprocal(rden[:, :, :], rden[:, :, :]))
                        me.wait()
                        o4 = o[:, :, 0:P].rearrange("p g (h c) -> p g h c", h=HPG)
                        r4 = rden[:, :, :].rearrange("p g (h c) -> p g h c", c=1).to_broadcast([P, G, HPG, HD])
                        nc.vector.tensor_tensor(o4, o4, r4, ALU.mult).then_inc(o_ready, 1)
                    if isinstance(t, int) and t == 1:
                        search_start()
                        count(0)
                    if first(t, 1) and not (isinstance(t, int) and t > NT):
                        dve.wait_ge(oT_hi_ready, b * NT + t)
                        nc.vector.tensor_tensor(k_lo[:, 1 - par, :], ps[:, 6, :], k_hi[:, 1 - par, :].bitcast(F32),
                                                ALU.subtract).then_inc(oT_ready, 1)
                    if isinstance(t, int) and t == NT - 1:
                        rank_marks()
                    if isinstance(t, int) and t == NT:
                        rank_chosen()
                    if isinstance(t, int) and t == NT + 1:
                        rank_number()
                    if first(t, 2):
                        dve.wait_ge(out_done, AHEAD + b * NT + t - 1)
                        dve.wait_ge(res_ready, b * NT + t - 1)
                        nc.vector.tensor_tensor(xo[:, par, :], ps[:, 4 + par, :], xo[:, par, :],
                                                ALU.add).then_inc(fin, 1)

                def dve_steps2():
                    for t in range(2):
                        step(t, t % 2)
                    with dve.Fori(0, (NT - 4) // 2) as j:
                        me.enter(j, N_PAIR)
                        for s in range(2):
                            step(j * 2 + (2 + s), s)
                        me.leave((NT - 4) // 2)
                    for t in range(NT - 2, NT + 2):
                        step(t, t % 2)

                dve_steps2()
                rank_split()

                me.leave(B)

            def list_head(e, b, turn):
                r = rank_hi[:, b, bass.ds(e, 1), :].rearrange("p e t -> p t e").to_broadcast([P, NT, 8])
                me.did(nc.vector.tensor_tensor(
                    one_hi[:, :, :], r,
                    con[:, C_EIGHT:C_TILE].rearrange("p (a c) -> p a c", a=1).to_broadcast([P, NT, 8]), ALU.is_equal))
                me.wait()
                dve.wait_ge(list_pe, AHEAD + turn * 4)
                me.did(nc.vector.tensor_tensor(
                    pay[:, :, 0:8], one_hi[:, :, :],
                    con[:, C_TILE:C_PCOL].rearrange("p (t a) -> p t a", a=1).to_broadcast([P, NT, 8]), ALU.mult))
                me.did(nc.vector.tensor_scalar(pay[:, :, 8:16], one_hi[:, :, :], con[:, C_PCOL:C_HEAD], None,
                                               ALU.mult))

            def list_part(e, b, turn, c):
                if c >= 2:
                    dve.wait_ge(list_pe, AHEAD + turn * 4 + c - 1)
                r = rank_lo[:, b, bass.ds(e, 1), c * 8:(c + 1) * 8].rearrange("p e t -> p t e").to_broadcast([P, 8, P])
                nc.vector.tensor_tensor(
                    one_lo[:, c % 2, :, :], r,
                    iota_bf[:, :].rearrange("p (a c) -> p a c", a=1).to_broadcast([P, 8, P]), ALU.is_equal
                ).then_inc(list_dve, 1)

            def list_tail(b, turn, copies):
                dve.wait_ge(list_pe, AHEAD + turn * 4 + 4)
                me.did(nc.vector.tensor_scalar(idx_f[:, :], ps[:, 4, 0:8], float(P), float(b * L), ALU.mult, ALU.add))
                me.wait()
                if copies is not None:
                    dve.wait_ge(idx_copied, copies)
                nc.vector.tensor_tensor(idx_next[:, b * SLOT_TILES:(b + 1) * SLOT_TILES], ps[:, 4, 8:16], idx_f[:, :],
                                        ALU.add).then_inc(idx_ready, 1)

            def w1_low(m, ready):
                dve.wait_ge(w1_hi_ready, ready)
                sl = slice(m * P, (m + 1) * P)
                nc.vector.tensor_tensor(w1_lo[:, :, sl], w1_raw[:, :, sl], w1_hi[:, :, sl].bitcast(F32),
                                        ALU.subtract).then_inc(w1_ready, 1)

            def rows_lo(unit, tt):
                dve.wait_ge(xi_hi_ready, unit * TPB + tt + 1)
                sl = slice(tt * P, (tt + 1) * P)
                nc.vector.tensor_tensor(xi_lo[:, :, sl], ps[:, 6 + tt % 2, :].rearrange("p (k c) -> p k c", k=KD),
                                        xi_hi[:, :, sl].bitcast(F32), ALU.subtract).then_inc(xi_ready, 1)

            for s in range(2):
                dve.wait_ge(out_stored[s], DMA_AHEAD + 16 * B * NT // 2)
                dve.wait_ge(xn_stored[s], 16 * (B * NBLK + 1))
            for b in range(B):
                list_head(0, b, b)
                for c in range(4):
                    list_part(0, b, b, c)
                list_tail(b, b, None)
            for m in range(2):
                w1_low(m, m + 1)
            for tt in range(TPB):
                rows_lo(0, tt)
            for m in range(2, KF):
                w1_low(m, m + 1)
            with dve.Fori(0, E) as e:
                me.enter(e, N_EXPERT)
                for u in range(UNITS):
                    n = e * UNITS + u
                    for m in range(KF):
                        dve.wait_ge(silu_done, AHEAD + n * KF + m + 1)
                        if m == 0:
                            dve.wait_ge(down_done, AHEAD + n * TPB)
                        me.did(nc.vector.tensor_copy(h_hi[:, m, :], hf[:, m % 2, :]))
                        me.wait()
                        nc.vector.tensor_tensor(h_lo[:, m, :], hf[:, m % 2, :], h_hi[:, m, :].bitcast(F32),
                                                ALU.subtract).then_inc(h_ready, 1)
                        if u == 0:
                            dve.wait_ge(w2_hi_ready, e * KF + m + 1)
                            nc.vector.tensor_tensor(w2_lo[:, m, :], w2_raw[:, m, :], w2_hi[:, m, :].bitcast(F32),
                                                    ALU.subtract).then_inc(w2_ready, 1)
                    turn = e * B + (B + u)
                    if u < B:
                        list_head(e + 1, u, turn)
                    for tt in range(TPB):
                        rows_lo(n + 1, tt)
                        if u < B:
                            list_part(e + 1, u, turn, tt)
                        if u == UNITS - 1:
                            for m in (2 * tt, 2 * tt + 1):
                                w1_low(m, e * KF + (KF + m + 1))
                    if u < B:
                        list_tail(u, turn, e + 1)
                me.leave(E)

        @block.tensor
        def _(pe):
            def product(dst, lhs, rhs, start, stop):
                (a_hi, a_lo), (b_hi, b_lo) = lhs, rhs
                nc.tensor.matmul(dst, a_hi, b_hi, start=start, stop=False, skip_group_check=True)
                nc.tensor.matmul(dst, a_hi, b_lo, start=False, stop=False, skip_group_check=True)
                return nc.tensor.matmul(dst, a_lo, b_hi, start=False, stop=stop, skip_group_check=True)

            def pair(ab, *where):
                return tuple(a[where] for a in ab)

            xT, wq, wo = (xT_hi, xT_lo), (wq_hi, wq_lo), (wo_hi, wo_lo)
            al = slice(None)

            def turn_x(j, t, bank=7):
                pe.wait_ge(xn_ready, j * TPB + (t + 1))
                if bank == 7 and not isinstance(j, int):
                    pe.wait_ge(xT_ready, j * TPB + t)
                for k in range(KD):
                    last = nc.tensor.transpose(ps[:, bank, k * P:(k + 1) * P], xn[:, t, k * P:(k + 1) * P], ident)
                last.then_inc(tr_done, 1)

            pe.wait_ge(table_in, 2 * 16)
            for t in range(TPB):
                turn_x(0, t, 4 + t)
            pe.wait_ge(w_ready, 1)
            pe.wait_ge(xT_ready, TPB)
            with pe.Fori(0, B) as b:
                for g in range(G):
                    nc.tensor.matmul(ps[:, g, 0:2 * VW], iota_bf[:, :], zero[:, :], start=True, stop=False,
                                     skip_group_check=True)
                def q_first(half):
                    cols = slice(half * HALF, (half + 1) * HALF)
                    for k in range(KD):
                        last = product(ps[:, 5, cols], pair(wq, al, k, slice(0, P)), pair(xT, al, k, cols),
                                       k == 0, k == KD - 1)
                    if half == 1:
                        last.then_inc(mm_done, 1)

                q_first(0)
                with pe.Fori(0, NBLK) as i:
                    n = b * NBLK + i
                    def kv(t):
                        par = t % 2
                        pe.wait_ge(k_ready, n * TPB + t + 1)
                        pe.wait_ge(vv_ready, AHEAD + n * TPB + t + 1)
                        for g in range(G):
                            cols = slice(g * P, (g + 1) * P)
                            last = product(ps[:, g, 0:2 * VW].rearrange("p (a c) -> p a c", a=2),
                                           pair((k_hi, k_lo), al, par, cols),
                                           pair((vv_hi, vv_lo), al, par, g, al, slice(0, VW)), False, False)
                        last.then_inc(kv_done, 1)

                    pe.wait_ge(xT_ready, (n + 1) * TPB)
                    q_first(1)
                    for m in range(1, KD):
                        if m == 1:
                            pe.wait_ge(lg_read, AHEAD + n * TPB)
                        elif m == 2:
                            pe.wait_ge(q_read, AHEAD + n * KD + 1)
                        else:
                            pe.wait_ge(k_read, AHEAD + n * TPB)
                        for k in range(KD):
                            last = product(ps[:, (5, 6, 5, 4)[m], :], pair(wq, al, k, slice(m * P, (m + 1) * P)),
                                           pair(xT, al, k, al), k == 0, k == KD - 1)
                        last.then_inc(mm_done, 1)
                    for t in range(TPB):
                        tok = slice(t * P, (t + 1) * P)
                        if t == 0:
                            pe.wait_ge(w_ready, 2)
                            pe.wait_ge(q_read, AHEAD + n * KD + 3)
                        else:
                            pe.wait_ge(v_read, AHEAD + n * TPB + t)
                            pe.wait_ge(lg_read, AHEAD + n * TPB + t)
                        for bank, cols in ((5, slice(2 * D, 2 * D + HALF)), (6, slice(2 * D + HALF, 3 * D + E))):
                            for k in range(KD):
                                last = product(ps[:, bank, 0:cols.stop - cols.start], pair(xT, al, k, tok),
                                               pair(wq, al, k, cols), k == 0, k == KD - 1)
                        last.then_inc(mm_done, 1)
                        if t in (0, TPB - 1):
                            turn_x(n + 1, t)
                        if t == 0:
                            pe.wait_ge(w_ready, 3)
                            pe.wait_ge(wo_ready, 1)
                            pe.wait_ge(q_read, AHEAD + n * KD + 4)
                        else:
                            pe.wait_ge(k_read, AHEAD + n * TPB + t)
                        for k in range(KD):
                            last = product(ps[:, 4, :], pair(xT, al, k, tok), pair(wq, al, k, slice(D, 2 * D)),
                                           k == 0, k == KD - 1)
                        last.then_inc(mm_done, 1)
                        if t in (1, 2):
                            turn_x(n + 1, t)
                        if t >= 1:
                            kv(t - 1)
                    pe.wait_ge(xT_ready, (n + 1) * TPB + 2)
                    pe.wait_ge(v_read, AHEAD + (n + 1) * TPB)
                    q_first(0)
                    kv(TPB - 1)

                def exchange(k):
                    pe.wait_ge(route_dve, b * ROUTE + k + 1)

                def step(t, par):
                    if not isinstance(t, int) or t < NT:
                        pe.wait_ge(q_ready, b * NT + t + 1)
                        pe.wait_ge(o_raw, AHEAD + b * NT + t)
                        qh, ql = q_part(vv_hi, par), q_part(vv_lo, par)
                        for g in range(G):
                            last = product(ps[:, g, 0:264].rearrange("p (a c) -> p a c", a=2), (qh[:, g, :], ql[:, g, :]),
                                           (sum_hi[:, g, :, :], sum_lo[:, g, :, :]), True, True)
                        last.then_inc(ctx_done, 1)
                    if first(t, 1) and not (isinstance(t, int) and t > NT):
                        pe.wait_ge(o_ready, b * NT + t)
                        if first(t, 2):
                            pe.wait_ge(oT_ready, b * NT + t - 1)
                        for g in range(G):
                            last = nc.tensor.transpose(ps[:, 6, g * P:(g + 1) * P], work[:, 1, g, 0:P], ident)
                        last.then_inc(otr_done, 1)
                    if isinstance(t, int) and t == NT:
                        exchange(BITS + 1)
                        nc.tensor.matmul(ps[:, 7, 0:4], same_block, cnt[:, 0:4], start=True, stop=True)
                        nc.tensor.matmul(ps[:, 7, 4:6], earlier, cnt[:, 2:4], start=True, stop=True
                                         ).then_inc(route_pe, 1)
                    if isinstance(t, int) and t == NT + 1:
                        exchange(BITS + 2)
                        nc.tensor.matmul(ps[:, 7, 0:2], earlier, cnt[:, 0:2], start=True, stop=True
                                         ).then_inc(route_pe, 1)
                    if first(t, 2):
                        pe.wait_ge(oT_ready, b * NT + t - 1)
                        pe.wait_ge(fin, AHEAD + b * NT + t - 2)
                        for k in range(KD):
                            last = product(ps[:, 4 + par, :], pair((k_hi, k_lo), al, par, slice(k * P, (k + 1) * P)),
                                           pair(wo, al, k, al), k == 0, k == KD - 1)
                        last.then_inc(out_done, 1)
                    if isinstance(t, int) and t == 1:
                        exchange(0)
                        for h in range(2):
                            last = nc.tensor.transpose(
                                ps[:, 7, h * P:(h + 1) * P],
                                probE[:, 4 * h:4 * h + 4, :].rearrange("p e t -> p (e t)"), ident)
                        last.then_inc(route_pe, 1)
                    if first(t, 1) and not (isinstance(t, int) and t > BITS):
                        exchange(t)
                        nc.tensor.matmul(ps[:, 7, 0:2], same_block, cnt[:, 0:2], start=True, stop=True
                                         ).then_inc(route_pe, 1)

                pe.wait_ge(sums_ready, b + 1)
                stage2_steps(pe, step)
                exchange(BITS + 3)
                for h in range(2):
                    last = nc.tensor.transpose(ps[:, 7, h * P:(h + 1) * P], mark[:, h, :], ident)
                last.then_inc(route_pe, 1)
                pe.wait_ge(fin, AHEAD + (b + 1) * NT)
                pe.wait_ge(rank_out, b + 1)

            def make_list(turn, c):
                if c == 0:
                    pe.wait_ge(idx_ready, AHEAD + turn)
                pe.wait_ge(list_dve, turn * 4 + (c + 1))
                for j in range(8):
                    last = nc.tensor.matmul(ps[:, 4, 0:16], one_lo[:, c % 2, j, :], pay[:, c * 8 + j, :],
                                            start=(c == 0 and j == 0), stop=(c == 3 and j == 7),
                                            skip_group_check=True)
                last.then_inc(list_pe, 1)

            def turn_rows(buf, loaded, before, tt):
                pe.wait_ge(rows_in[buf], loaded)
                if before is not None:
                    pe.wait_ge(xi_ready, before)
                for k in range(KD):
                    last = nc.tensor.transpose(ps[:, 6 + tt % 2, k * P:(k + 1) * P],
                                               rows[:, buf, tt, k * P:(k + 1) * P], ident)
                last.then_inc(gtr_done, 1)

            for b in range(B):
                for c in range(4):
                    make_list(b, c)
            for tt in range(TPB):
                turn_rows(0, 64, tt - 1 if tt >= 2 else None, tt)
            xi, w1s, w2s, hs = (xi_hi, xi_lo), (w1_hi, w1_lo), (w2_hi, w2_lo), (h_hi, h_lo)
            with pe.Fori(0, E) as e:
                for u in range(UNITS):
                    n = e * UNITS + u
                    pe.wait_ge(xi_ready, (n + 1) * TPB)
                    for m in range(KF):
                        if u == 0:
                            pe.wait_ge(w1_ready, e * KF + (m + 1))
                        pe.wait_ge(silu_done, AHEAD + n * KF + max(m - 1, 0))
                        for k in range(KD):
                            last = product(ps[:, m % 2, :], pair(w1s, al, k, slice(m * P, (m + 1) * P)),
                                           pair(xi, al, k, al), k == 0, k == KD - 1)
                        last.then_inc(up_done, 1)
                    for tt in range(TPB):
                        turn_rows((u + 1) % 2, e * 128 + ((u + 1) // 2 + 1) * 64, (n + 1) * TPB + (tt - 1), tt)
                        pe.wait_ge(y_ready, AHEAD + n * TPB + max(tt - 1, 0))
                        for k in range(KF):
                            if tt == 0:
                                pe.wait_ge(h_ready, AHEAD + n * KF + (k + 1))
                                if u == 0:
                                    pe.wait_ge(w2_ready, e * KF + (k + 1))
                            last = product(ps[:, 2 + tt % 2, :], pair(hs, al, k, slice(tt * P, (tt + 1) * P)),
                                           pair(w2s, al, k, al), k == 0, k == KF - 1)
                        last.then_inc(down_done, 1)
                        if u < B:
                            make_list(e * B + (B + u), tt)


_INS = ['L0_attn_x', 'L0_attn_W_qkv', 'L0_attn_b_qkv', 'L0_attn_W_out', 'L0_attn_b_out', 'L0_ffn_choice_w',
        'L0_ffn_w1', 'L0_ffn_w2']


def kernel(**inputs):
    import concourse.bacc as bacc
    from concourse.bass_utils import run_bass_kernel_spmd as run

    nc = bacc.Bacc("TRN2", target_bir_lowering=False, num_devices=1)
    arrays, args = {}, []
    table, bits = constants()
    for name, a in [(n, np.ascontiguousarray(inputs[n])) for n in _INS] + [("consts", table), ("bits", bits)]:
        arrays[f"in_{name}_dram"] = a
        args.append(nc.dram_tensor(f"in_{name}_dram", a.shape, mybir.dt.from_np(a.dtype), kind="ExternalInput").ap())
    args.append(nc.dram_tensor("out_0_dram", (B, L, D), F32, kind="ExternalOutput").ap())
    args.append(nc.dram_tensor("normed_rows", (B * L, ROW), F32, kind="Internal").ap())
    build(nc, *args)
    r = run(nc, [arrays], core_ids=[0])
    return r.results[0]["out_0_dram"]
```
